# Optimizing a Trainium2 kernel written in Bass

```python
import numpy as np
import jax
import jax.numpy as jnp

def _softmax(x, axis=-1):
    return jax.nn.softmax(x, axis=axis)

def _gelu(x):
    return jax.nn.gelu(x, approximate=True)

def _silu(x):
    return jax.nn.silu(x)

def _sigmoid(x):
    return jax.nn.sigmoid(x)

def _layernorm(x, axis=-1, eps=1e-05):
    m = jnp.mean(x, axis=axis, keepdims=True)
    v = jnp.var(x, axis=axis, keepdims=True)
    return (x - m) / jnp.sqrt(v + eps)

def _scatter_add(tgt, idx, src, axis=0):
    return tgt.at[idx].add(src)

def _segment_sum(src, seg, n):
    return jax.ops.segment_sum(src, seg, n)
kernel_name = 'mk_decoder_preln_d1_seqx_r4_a85ea0'

def setup_inputs(seed: int=0):
    np.random.seed(seed)
    _w = jnp.asarray

    def _rec_inputs():
        import jax
        import jax.numpy as jnp
        _rk = jax.random.key(seed)
        x = -0.0002928 + 1 * jax.random.normal(jax.random.fold_in(_rk, 1), (16, 128, 256), jnp.float32)
        _lenS = 128 - jax.random.randint(jax.random.fold_in(_rk, 7), (16,), 0, max(1, 128 // 4) + 1, jnp.int32)
        _lenS2 = 128 - jax.random.randint(jax.random.fold_in(_rk, 8), (16,), 0, max(1, 128 // 4) + 1, jnp.int32)
        _ctx_1024P = jax.random.normal(jax.random.fold_in(_rk, 11), (16, 16, 256), jnp.float32)
        _ctx_1024c = jax.random.dirichlet(jax.random.fold_in(_rk, 511), 0.3 * jnp.ones((16,), jnp.float32), (16, 128))
        _ctx_1024t = jnp.einsum('bsk,bkd->bsd', _ctx_1024c, _ctx_1024P)
        _ctx_1024t = _ctx_1024t * jax.lax.rsqrt(jnp.mean(jnp.square(_ctx_1024t)) + 1e-12) * 0.953939
        ctx_1024 = 4.13588e-05 + 0.999923 * (_ctx_1024t + 0.3 * jax.random.normal(jax.random.fold_in(_rk, 611), (16, 128, 256), jnp.float32))
        return (x, ctx_1024)
    x, ctx_1024 = _rec_inputs()

    def _L0_attn_setup():
        import jax, jax.numpy as jnp
        import numpy as np
        HEADS = 16
        HEAD_DIM = 64
        EMB = 256
        B, S = (4, 512)
        SCALE = 1.0 / 8.0
        MASK_PENALTY = -50.0
        key = jax.random.key(seed)
        ks = jax.random.split(key, 5)
        x = jax.random.normal(ks[0], (B, S, EMB), dtype=jnp.float32)
        Wq = jax.random.normal(ks[1], (EMB, HEADS * HEAD_DIM), dtype=jnp.float32) * 0.02
        Wk = jax.random.normal(ks[2], (EMB, HEADS * HEAD_DIM), dtype=jnp.float32) * 0.02
        Wv = jax.random.normal(ks[3], (EMB, HEADS * HEAD_DIM), dtype=jnp.float32) * 0.02
        Wr = jax.random.normal(ks[4], (HEADS * HEAD_DIM, EMB), dtype=jnp.float32) * 0.02
        return {'x': x, 'Wq': Wq, 'Wk': Wk, 'Wv': Wv, 'Wr': Wr}
    _L0_attn_all = _L0_attn_setup()
    _L0_attn_in = {k: v for k, v in _L0_attn_all.items() if k in ('Wq', 'Wk', 'Wv', 'Wr')}
    del _L0_attn_all

    def _L0_xattn_setup():
        import jax, jax.numpy as jnp
        import numpy as np
        HIDDEN = 256
        HEADS = 16
        HEAD_DIM = 64
        key = jax.random.key(seed)
        ks = jax.random.split(key, 7)
        B, Q, K = (2, 512, 1024)
        s = 1.0 / np.sqrt(HIDDEN)
        return {'query': jax.random.normal(ks[0], (B, Q, HIDDEN), dtype=jnp.float32), 'key': jax.random.normal(ks[1], (B, K, HIDDEN), dtype=jnp.float32), 'value': jax.random.normal(ks[2], (B, K, HIDDEN), dtype=jnp.float32), 'w_q': jax.random.normal(ks[3], (HIDDEN, HEADS * HEAD_DIM), dtype=jnp.float32) * s, 'w_k': jax.random.normal(ks[4], (HIDDEN, HEADS * HEAD_DIM), dtype=jnp.float32) * s, 'w_v': jax.random.normal(ks[5], (HIDDEN, HEADS * HEAD_DIM), dtype=jnp.float32) * s, 'w_o': jax.random.normal(ks[6], (HEADS * HEAD_DIM, HIDDEN), dtype=jnp.float32) * s}
    _L0_xattn_all = _L0_xattn_setup()
    _L0_xattn_in = {k: v for k, v in _L0_xattn_all.items() if k in ('w_q', 'w_k', 'w_v', 'w_o')}
    del _L0_xattn_all

    def _L0_ffn_setup():
        import jax, jax.numpy as jnp
        import numpy as np
        MODEL_DIM = 256
        HIDDEN = 512
        NUM_GROUPS = 2
        EXPERTS_PER_GP = 4
        NUM_EXPERTS = NUM_GROUPS * EXPERTS_PER_GP
        TOP_K = 2
        B, T = (2, 512)

        def _swiglu(x):
            a, b = jnp.split(x, 2, axis=-1)
            return jax.nn.silu(a) * b
        key = jax.random.key(seed)
        ks = jax.random.split(key, 7)
        s = 0.02
        return {'x': jax.random.normal(ks[0], (B, T, MODEL_DIM), jnp.float32), 'w_in': jax.random.normal(ks[1], (HIDDEN * 2, MODEL_DIM), jnp.float32) * s, 'w_out': jax.random.normal(ks[2], (MODEL_DIM, HIDDEN), jnp.float32) * s, 'w1': jax.random.normal(ks[3], (HIDDEN * 2, MODEL_DIM), jnp.float32) * s, 'w2': jax.random.normal(ks[4], (NUM_EXPERTS, MODEL_DIM, HIDDEN), jnp.float32) * s, 'wg': jax.random.normal(ks[5], (NUM_GROUPS, MODEL_DIM), jnp.float32) * s, 'we': jax.random.normal(ks[6], (NUM_EXPERTS, MODEL_DIM), jnp.float32) * s, 'gb': jnp.zeros((NUM_GROUPS,), jnp.float32), 'eb': jnp.zeros((NUM_EXPERTS,), jnp.float32)}
    _L0_ffn_all = _L0_ffn_setup()
    _L0_ffn_in = {k: v for k, v in _L0_ffn_all.items() if k in ('w_in', 'w_out', 'w1', 'w2', 'wg', 'we', 'gb', 'eb')}
    del _L0_ffn_all
    return {'x': x, 'ctx_1024': ctx_1024, 'L0_attn_Wq': _L0_attn_in['Wq'], 'L0_attn_Wk': _L0_attn_in['Wk'], 'L0_attn_Wv': _L0_attn_in['Wv'], 'L0_attn_Wr': _L0_attn_in['Wr'], 'L0_xattn_w_q': _L0_xattn_in['w_q'], 'L0_xattn_w_k': _L0_xattn_in['w_k'], 'L0_xattn_w_v': _L0_xattn_in['w_v'], 'L0_xattn_w_o': _L0_xattn_in['w_o'], 'L0_ffn_w_in': _L0_ffn_in['w_in'], 'L0_ffn_w_out': _L0_ffn_in['w_out'], 'L0_ffn_w1': _L0_ffn_in['w1'], 'L0_ffn_w2': _L0_ffn_in['w2'], 'L0_ffn_wg': _L0_ffn_in['wg'], 'L0_ffn_we': _L0_ffn_in['we'], 'L0_ffn_gb': _L0_ffn_in['gb'], 'L0_ffn_eb': _L0_ffn_in['eb']}

def reference(x, ctx_1024, L0_attn_Wq, L0_attn_Wk, L0_attn_Wv, L0_attn_Wr, L0_xattn_w_q, L0_xattn_w_k, L0_xattn_w_v, L0_xattn_w_o, L0_ffn_w_in, L0_ffn_w_out, L0_ffn_w1, L0_ffn_w2, L0_ffn_wg, L0_ffn_we, L0_ffn_gb, L0_ffn_eb):
    import jax
    import jax.numpy as jnp

    def _L0_attn_ref(x, Wq, Wk, Wv, Wr):
        import jax, jax.numpy as jnp
        import numpy as np
        HEADS = 16
        HEAD_DIM = 64
        EMB = 256
        B, S = (4, 512)
        SCALE = 1.0 / 8.0
        MASK_PENALTY = -50.0
        b, s, _ = x.shape
        q = (x @ Wq).reshape(b, s, HEADS, HEAD_DIM)
        k = (x @ Wk).reshape(b, s, HEADS, HEAD_DIM)
        v = (x @ Wv).reshape(b, s, HEADS, HEAD_DIM)
        scores = SCALE * jnp.einsum('bqhd,bkhd->bhqk', q, k)
        causal = jnp.triu(jnp.ones((s, s), dtype=x.dtype), k=1)
        scores = scores + MASK_PENALTY * causal
        attn = jax.nn.softmax(scores, axis=-1)
        out = jnp.einsum('bhqk,bkhd->bqhd', attn, v).reshape(b, s, HEADS * HEAD_DIM)
        return out @ Wr

    def _L0_xattn_ref(query, key, value, w_q, w_k, w_v, w_o):
        import jax, jax.numpy as jnp
        import numpy as np
        HIDDEN = 256
        HEADS = 16
        HEAD_DIM = 64
        B, Q, _ = query.shape
        Kl = key.shape[1]
        scale = HEAD_DIM ** (-0.5)
        q = (query @ w_q).reshape(B, Q, HEADS, HEAD_DIM).transpose(0, 2, 1, 3)
        k = (key @ w_k).reshape(B, Kl, HEADS, HEAD_DIM).transpose(0, 2, 1, 3)
        v = (value @ w_v).reshape(B, Kl, HEADS, HEAD_DIM).transpose(0, 2, 1, 3)
        scores = jnp.einsum('bhqd,bhkd->bhqk', q, k) * scale
        attn = jax.nn.softmax(scores, axis=-1)
        out = jnp.einsum('bhqk,bhkd->bhqd', attn, v)
        out = out.transpose(0, 2, 1, 3).reshape(B, Q, HEADS * HEAD_DIM)
        return out @ w_o

    def _L0_ffn_ref(x, w_in, w_out, w1, w2, wg, we, gb, eb):
        import jax, jax.numpy as jnp
        import numpy as np
        MODEL_DIM = 256
        HIDDEN = 512
        NUM_GROUPS = 2
        EXPERTS_PER_GP = 4
        NUM_EXPERTS = NUM_GROUPS * EXPERTS_PER_GP
        TOP_K = 2
        B, T = (2, 512)

        def _swiglu(x):
            a, b = jnp.split(x, 2, axis=-1)
            return jax.nn.silu(a) * b
        Bs, Ts, C = x.shape
        S = Bs * Ts
        flat = x.reshape(S, C)
        shared = _swiglu(flat @ w_in.T) @ w_out.T
        g_probs = jax.nn.softmax(flat @ wg.T + gb, axis=-1)
        g_idx = jnp.argmax(g_probs, axis=-1)
        e_logits = flat @ we.T + eb
        egid = jnp.arange(NUM_EXPERTS) // EXPERTS_PER_GP
        masked = jnp.where(g_idx[:, None] == egid[None, :], e_logits, -jnp.inf)
        e_probs = jax.nn.softmax(masked, axis=-1)
        g_prob = jnp.take_along_axis(g_probs, g_idx[:, None], axis=1)
        p_expert = e_probs * g_prob
        topv, topi = jax.lax.top_k(p_expert, TOP_K)
        w_se = jnp.zeros((S, NUM_EXPERTS), x.dtype).at[jnp.arange(S)[:, None], topi].add(topv)
        h = _swiglu(flat @ w1.T)
        routed = jnp.zeros_like(shared)
        for e in range(NUM_EXPERTS):
            routed = routed + h * w_se[:, e:e + 1] @ w2[e].T
        return (shared + routed).reshape(Bs, Ts, C)
    x = x + _L0_attn_ref(_layernorm(x, axis=-1), L0_attn_Wq, L0_attn_Wk, L0_attn_Wv, L0_attn_Wr)
    x = x + _L0_xattn_ref(_layernorm(x, axis=-1), ctx_1024, ctx_1024, L0_xattn_w_q, L0_xattn_w_k, L0_xattn_w_v, L0_xattn_w_o)
    x = x + _L0_ffn_ref(_layernorm(x, axis=-1), L0_ffn_w_in, L0_ffn_w_out, L0_ffn_w1, L0_ffn_w2, L0_ffn_wg, L0_ffn_we, L0_ffn_gb, L0_ffn_eb)
    return x

_drawn_inputs = setup_inputs


def setup_inputs(seed=0):
    import zlib

    import numpy as np

    out = dict(_drawn_inputs(seed))
    spreads = {'L0_ffn_gb': (0.0, 0.8), 'L0_ffn_eb': (0.0, 0.8)}
    factors = {'L0_attn_Wq': 8.0,
     'L0_attn_Wk': 8.0,
     'L0_ffn_w_in': 3.303,
     'L0_ffn_w_out': 3.15,
     'L0_ffn_w1': 8.0,
     'L0_ffn_w2': 8.0,
     'L0_ffn_wg': 8.0,
     'L0_ffn_we': 8.0}
    for name, (base, spread) in spreads.items():
        noise = np.random.default_rng([zlib.crc32(name.encode()), seed]).standard_normal(out[name].shape)
        drawn = base * np.exp(spread * noise) if base else spread * noise
        out[name] = jnp.asarray(drawn.astype(out[name].dtype))
    for name, factor in factors.items():
        out[name] = (out[name] * factor).astype(out[name].dtype)
    return out
```

```python
from contextlib import ExitStack

import concourse.bass as bass
from concourse import mybir

F32 = mybir.dt.float32
F32R = mybir.dt.float32r
BF16 = mybir.dt.bfloat16
ACT = mybir.ActivationFunctionType
ALU = mybir.AluOpType
AX = mybir.AxisListType

P = 128
B, S, D = 16, 128, 256
HEADS, HD = 16, 64
INNER = HEADS * HD
HID = 512
GROUPS, PER_GROUP = 2, 4
NE = GROUPS * PER_GROUP
NG = GROUPS + NE
TOP_K = 2
EPS = 1e-5
MASK = -50.0
SCALE = HD ** -0.5

TPG = 4
GT = TPG * P
NGRP = B // TPG
KT = D // P
PAIRS = HEADS // 2
HT = HID // P
VP = HD + 1
HALF = HEADS // 2
CHUNK = KT * INNER
STAGES = 3
FIN = 2
OUTS = NE // 2 + 1


def build(nc, x, ctxT, wq, wk, wv, wr, xq, xk, xv, xr, w1, win, wout, w2, wgate, bgate, out):
    ctx = ExitStack()
    with ctx:
        def sem(name):
            return ctx.enter_context(nc.semaphore(name))

        def sb(name, shape, dt=F32, stack=ctx):
            return stack.enter_context(nc.sbuf_tensor(name, shape, dt))

        def ps(name):
            return ctx.enter_context(nc.psum_tensor(name, [P, 2, 512], F32))

        xres = sb("xres", [P, B, D])
        stage = sb("stage", [P, STAGES, CHUNK])
        ident = sb("ident", [P, P])
        identb = sb("identb", [P, P], BF16)
        maskb = sb("maskb", [P, TPG, P], BF16)
        z = sb("z", [P, TPG, D])
        zhi = sb("zhi", [P, KT, GT], F32R)
        zlo = sb("zlo", [P, KT, GT], F32R)
        bnst = sb("bnst", [P, TPG, 6])
        mv = sb("mv", [P, TPG, 2])
        veps = sb("veps", [P, TPG])
        rstd = sb("rstd", [P, TPG])
        mhalf = sb("mhalf", [P, TPG])
        eps = sb("eps", [P, TPG])
        psS, psW, psT, psA = ps("psS"), ps("psW"), ps("psT"), ps("psA")

        x_in = [sem(f"x_in{g}") for g in range(NGRP)]
        stage_in = [sem(f"stage_in{k}") for k in range(STAGES)]
        gate_in, ctx_in = sem("gate_in"), sem("ctx_in")
        zeroed, consts, ffn_ones, ffn_consts = sem("zeroed"), sem("consts"), sem("ffn_ones"), sem("ffn_consts")
        w_hi, w_lo = sem("w_hi"), sem("w_lo")
        c_hi, c_lo = sem("c_hi"), sem("c_lo")
        bn_done, bn_seen, mv_done, eps_done, rstd_done, z_done = (
            sem("bn_done"), sem("bn_seen"), sem("mv_done"), sem("eps_done"), sem("rstd_done"), sem("z_done"))
        zT_mm, z_hi, z_lo = sem("zT_mm"), sem("z_hi"), sem("z_lo")
        qk_mm, qk_hi, qk_lo = sem("qk_mm"), sem("qk_hi"), sem("qk_lo")
        v_mm, v_done = sem("v_mm"), sem("v_done")
        s_mm, max_done, exp_done = sem("s_mm"), sem("max_done"), sem("exp_done")
        pT_mm, pT0_done, pT1_done = sem("pT_mm"), sem("pT0_done"), sem("pT1_done")
        av_mm, recip_done, o_done = sem("av_mm"), sem("recip_done"), sem("o_done")
        oT_mm, oT_hi, oT_lo = sem("oT_mm"), sem("oT_hi"), sem("oT_lo")
        proj_mm, res_done = sem("proj_mm"), sem("res_done")
        gate_mm, gate_copied, gate_step, gate_exp, wse_done = (
            sem("gate_mm"), sem("gate_copied"), sem("gate_step"), sem("gate_exp"), sem("wse_done"))
        ab_mm, silu_done, h_done, h_hi, h_lo = (
            sem("ab_mm"), sem("silu_done"), sem("h_done"), sem("h_hi"), sem("h_lo"))
        out_mm, out_used, acc_done, fin_done = sem("out_mm"), sem("out_used"), sem("acc_done"), sem("fin_done")
        stored = [sem(f"stored{i}") for i in range(FIN)]

        def flat(ap):
            return ap.rearrange("p a b -> p (a b)")

        def rows(g):
            return xres[:, bass.ds(g * TPG, TPG), :]

        def row_tile(g, t):
            return flat(xres[:, bass.ds(g * TPG + t, 1), :])

        def product(o, lhs, rhs, start, stop, **kw):
            (lh, ll), (rh, rl) = lhs, rhs
            nc.tensor.matmul(o, lh, rl, start=start, stop=False, **kw)
            nc.tensor.matmul(o, lh, rh, start=False, stop=False, **kw)
            return nc.tensor.matmul(o, ll, rh, start=False, stop=stop, **kw)

        def ln_stats(dve, g, row_g):
            for t in range(TPG):
                nc.vector.bn_stats(bnst[:, t, :], row_tile(row_g, t)).then_inc(bn_done, 1)
            dve.wait_ge(bn_done, (g + 1) * TPG)
            dve.sem_inc(bn_seen, 1)
            for t in range(TPG):
                nc.vector.bn_aggr(mv[:, t, :], bnst[:, t, :]).then_inc(mv_done, 1)

        def ln_rows(dve, g, row_g):
            dve.wait_ge(rstd_done, g + 1)
            if not (isinstance(g, int) and g == 0):
                dve.wait_ge(zT_mm, g * KT)
            for t in range(TPG):
                nc.vector.tensor_scalar(z[:, t, :], row_tile(row_g, t), mv[:, t, 0:1], rstd[:, t:t + 1],
                                        ALU.subtract, ALU.mult).then_inc(z_done, 1)

        def ln_scale(pool, first, end):
            with pool.Fori(first, end) as g:
                pool.wait_ge(mv_done, (g + 1) * TPG)
                nc.gpsimd.tensor_tensor(veps[:], mv[:, :, 1], eps[:], ALU.add).then_inc(eps_done, 1)
                pool.wait_ge(eps_done, g + 1)
                nc.gpsimd.tensor_tensor(rstd[:], veps[:], mhalf[:], ALU.pow).then_inc(rstd_done, 1)

        def z_transposes(pe, g, banks):
            pe.wait_ge(z_done, (g + 1) * TPG)
            for k in range(KT):
                for t in range(TPG):
                    mm = nc.tensor.transpose(banks[:, k, t * P:(t + 1) * P], z[:, t, k * P:(k + 1) * P], ident[:])
                mm.then_inc(zT_mm, 1)

        def z_split_hi(act, g, banks):
            for k in range(KT):
                act.wait_ge(zT_mm, g * KT + k + 1)
                nc.scalar.activation(zhi[:, k, :], banks[:, k, :], ACT.Copy).then_inc(z_hi, 1)

        def z_split_lo(dve, g, banks):
            for k in range(KT):
                dve.wait_ge(z_hi, g * KT + k + 1)
                nc.vector.tensor_tensor(zlo[:, k, :], banks[:, k, :], zhi[:, k, :].bitcast(F32),
                                        ALU.subtract).then_inc(z_lo, 1)

        def piece(n, size):
            return stage[:, n % STAGES, 0:size]

        def weights_hi(act, n, dst, size, scale=1.0):
            act.wait_ge(stage_in[n % STAGES], 16 * (n // STAGES + 1))
            nc.scalar.activation(dst, piece(n, size), ACT.Copy, scale=scale).then_inc(w_hi, 1)

        def weights_lo(dve, n, dst, hi, size, scale=1.0):
            dve.wait_ge(w_hi, n + 1)
            nc.vector.scalar_tensor_tensor(dst, piece(n, size), scale, hi.bitcast(F32),
                                           ALU.mult, ALU.subtract).then_inc(w_lo, 1)

        def cols(w, k):
            return w.rearrange("(k p) n -> p k n", p=P), k

        pieces = [cols(w, k) for w, k in
                  [(wq, KT), (wk, KT), (wv, KT), (wr, PAIRS), (xq, KT), (xk, KT), (xv, KT), (xr, PAIRS),
                   (w1, KT), (win, KT), (wout, HT)]]
        w2_rows = w2.rearrange("(k p) n -> k p n", p=P)
        N_ATT, N_FFN = 4, 3 + HT

        att = ExitStack()
        with att:
            def ab(name, shape, dt=F32):
                return sb(name, shape, dt, att)

            wh = [ab(f"w{n}_hi", [P, KT, INNER], F32R) for n in "qkv"]
            wl = [ab(f"w{n}_lo", [P, KT, INNER], F32R) for n in "qkv"]
            wo_hi = ab("wo_hi", [P, PAIRS, D], F32R)
            wo_lo = ab("wo_lo", [P, PAIRS, D], F32R)
            craw = ab("craw", [P, KT, GT])
            chi = ab("chi", [P, KT, GT], F32R)
            clo = ab("clo", [P, KT, GT], F32R)
            qkhi = ab("qkhi", [P, 2, 2, GT], F32R)
            qklo = ab("qklo", [P, 2, 2, GT], F32R)
            v = ab("v", [P, TPG, HEADS, VP])
            nmax = ab("nmax", [P, 2, TPG])
            prob = ab("prob", [P, 2, TPG, P])
            probT = ab("probT", [P, 2, GT])
            rsum = ab("rsum", [P, 2, TPG])
            o = ab("o", [P, TPG, 2 * HD])
            othi = ab("othi", [P, GT], F32R)
            otlo = ab("otlo", [P, GT], F32R)
            whole = [(t[:].rearrange("p a b -> p (a b)")) for t in (*wh, wo_hi)]
            whole_lo = [(t[:].rearrange("p a b -> p (a b)")) for t in (*wl, wo_lo)]
            scales = [SCALE, 1.0, 1.0, 1.0]
            Q, K, V = 0, 1, 2

            block = att.enter_context(nc.Block())

            @block.sync
            def _(sp):
                xv_ = x.rearrange("(g t p) d -> g p t d", p=P, t=TPG)
                sp.dma_start(xres[:, 0:TPG, :], xv_[0]).then_inc(x_in[0], 16)

                def load(n):
                    if n >= STAGES:
                        sp.wait_ge(w_lo, n - STAGES + 1)
                    src, k = pieces[n]
                    sp.dma_start(piece(n, CHUNK).rearrange("p (k n) -> p k n", k=k), src)\
                        .then_inc(stage_in[n % STAGES], 16)

                for n in range(N_ATT - 1):
                    load(n)
                for g in range(1, NGRP):
                    sp.dma_start(xres[:, g * TPG:(g + 1) * TPG, :], xv_[g]).then_inc(x_in[g], 16)
                ctx_v = ctxT.rearrange("(k p) t -> p k t", p=P)
                sp.dma_start(craw[:], ctx_v[:, :, 0:GT]).then_inc(ctx_in, 16)
                for n in range(N_ATT - 1, 2 * N_ATT):
                    load(n)
                for g in range(1, NGRP):
                    sp.wait_ge(c_lo, g)
                    sp.dma_start(craw[:], ctx_v[:, :, g * GT:(g + 1) * GT]).then_inc(ctx_in, 16)

            @block.gpsimd
            def _(pool):
                nc.gpsimd.memset(ident[:], 0.0).then_inc(zeroed, 1)
                nc.gpsimd.memset(identb[:], 0.0).then_inc(zeroed, 1)
                nc.gpsimd.memset(maskb[:], 0.0).then_inc(zeroed, 1)
                nc.gpsimd.memset(mhalf[:], -0.5).then_inc(consts, 1)
                nc.gpsimd.memset(eps[:], EPS).then_inc(consts, 1)
                nc.gpsimd.memset(v[:, :, :, HD:VP], 1.0).then_inc(consts, 1)
                pool.wait_ge(zeroed, 3)
                for m in (ident, identb):
                    nc.gpsimd.affine_select(out=m[:], in_=m[:], compare_op=ALU.not_equal, fill=1.0, base=0,
                                            pattern=[[-1, P]], channel_multiplier=1).then_inc(consts, 1)
                nc.gpsimd.affine_select(out=maskb[:], in_=maskb[:], compare_op=ALU.is_ge, fill=MASK, base=0,
                                        pattern=[[0, TPG], [-1, P]], channel_multiplier=1).then_inc(consts, 1)
                pool.wait_ge(consts, 6)
                ln_scale(pool, 0, 2 * NGRP)

            @block.scalar
            def _(act):
                act.preload_act_table(ACT.Exp)

                def split_context(g, cg):
                    act.wait_ge(ctx_in, (cg + 1) * 16)
                    nc.scalar.activation(flat(chi[:]), flat(craw[:]), ACT.Copy).then_inc(c_hi, 1)

                def qk_split(G, j):
                    s2 = G * 2 * PAIRS + 2 * j
                    for n in range(2):
                        act.wait_ge(qk_mm, s2 + n + 1)
                        nc.scalar.activation(qkhi[:, j % 2, n, :], psW[:, n, :], ACT.Copy).then_inc(qk_hi, 1)

                def v_copy(G, half, t, bank):
                    act.wait_ge(v_mm, G * 2 * TPG + half * TPG + t + 1)
                    nc.scalar.activation(v[:, t, half * HALF:(half + 1) * HALF, 0:HD],
                                         psW[:, bank, :].rearrange("p (h d) -> p h d", d=HD), ACT.Copy).then_inc(v_done, 1)

                def oT_split(s):
                    act.wait_ge(oT_mm, s)
                    nc.scalar.activation(othi[:], psT[:, 0, :], ACT.Copy).then_inc(oT_hi, 1)

                def step(ph, G, j, first=False, more=True):
                    s = G * PAIRS + j
                    if not first:
                        oT_split(s)
                    for h in range(2):
                        act.wait_ge(max_done, 2 * s + h + 1)
                        if not (isinstance(s, int) and s == 0):
                            act.wait_ge(pT_mm, 2 * s)
                        for b in range(TPG):
                            e = nc.scalar.activation(prob[:, h, b, :], psS[:, h, b * P:(b + 1) * P], ACT.Exp,
                                                     bias=nmax[:, h, b:b + 1])
                        e.then_inc(exp_done, 1)
                    act.wait_ge(pT_mm, 2 * s + 1)
                    nc.scalar.activation(probT[:, 0, :], psT[:, 0, :], ACT.Copy).then_inc(pT0_done, 1)
                    if j + 1 < PAIRS or more:
                        qk_split(G, j + 1)
                    if j < TPG:
                        v_copy(G, 1, j, 0)
                    if j == PAIRS - 2 and more:
                        z_split_hi(act, G + 1, psW)
                        if ph == 1:
                            split_context(G + 1, G + 1 - NGRP)
                    if j == PAIRS - 1 and more:
                        for t in range(TPG):
                            v_copy(G + 1, 0, t, t % 2)

                for ph in range(2):
                    G0 = ph * NGRP
                    if ph == 1:
                        act.wait_ge(proj_mm, G0 * PAIRS)
                        split_context(G0, 0)
                    for n in range(N_ATT):
                        weights_hi(act, ph * N_ATT + n, whole[n], CHUNK, scales[n])
                    z_split_hi(act, G0, psW)
                    qk_split(G0, 0)
                    for t in range(TPG):
                        v_copy(G0, 0, t, t % 2)
                    step(ph, G0, 0, first=True)
                    with act.Fori(G0, G0 + NGRP - 1) as G:
                        for j in range(1, PAIRS):
                            step(ph, G, j)
                        step(ph, G + 1, 0)
                    for j in range(1, PAIRS):
                        step(ph, G0 + NGRP - 1, j, more=False)
                    oT_split((G0 + NGRP) * PAIRS)

            @block.vector
            def _(dve):
                def qk_split(G, j):
                    s2 = G * 2 * PAIRS + 2 * j
                    for n in range(2):
                        dve.wait_ge(qk_hi, s2 + n + 1)
                        nc.vector.tensor_tensor(qklo[:, j % 2, n, :], psW[:, n, :], qkhi[:, j % 2, n, :].bitcast(F32),
                                                ALU.subtract).then_inc(qk_lo, 1)

                def oT_split(s):
                    dve.wait_ge(oT_hi, s)
                    nc.vector.tensor_tensor(otlo[:], psT[:, 0, :], othi[:].bitcast(F32),
                                            ALU.subtract).then_inc(oT_lo, 1)

                def split_context(cg):
                    dve.wait_ge(c_hi, cg + 1)
                    nc.vector.tensor_tensor(flat(clo[:]), flat(craw[:]), flat(chi[:]).bitcast(F32),
                                            ALU.subtract).then_inc(c_lo, 1)

                def residual(ph, G):
                    dve.wait_ge(proj_mm, (G + 1) * PAIRS)
                    for i in range(2):
                        half = flat(xres[:, bass.ds(row_group(ph, G) * TPG + 2 * i, 2), :])
                        r = nc.vector.tensor_tensor(half, psA[:, i, :], half, ALU.add)
                    r.then_inc(res_done, 1)

                def row_group(ph, G):
                    return G - ph * NGRP

                def step(ph, G, j, first=False, more=True):
                    s = G * PAIRS + j
                    dve.wait_ge(s_mm, s + 1)
                    for h in range(2):
                        nc.vector.tensor_reduce(nmax[:, h, :], psS[:, h, :].rearrange("p (b k) -> p b k", k=P),
                                                AX.X, ALU.max, negate=True).then_inc(max_done, 1)
                    if not first:
                        oT_split(s)
                    if j == 1 and more:
                        ln_stats(dve, G + 1, row_group(ph, G + 1))
                    dve.wait_ge(pT_mm, 2 * s + 2)
                    nc.vector.tensor_copy(probT[:, 1, :], psT[:, 1, :]).then_inc(pT1_done, 1)
                    if j + 1 < PAIRS or more:
                        qk_split(G, j + 1)
                    if j == 3 and more:
                        ln_rows(dve, G + 1, row_group(ph, G + 1))
                    av = [psS[:, h, 0:TPG * VP].rearrange("p (b d) -> p b d", d=VP) for h in range(2)]
                    for h in range(2):
                        dve.wait_ge(av_mm, 2 * s + h + 1)
                        nc.vector.reciprocal(rsum[:, h, :], av[h][:, :, HD]).then_inc(recip_done, 1)
                    for h in range(2):
                        dve.wait_ge(recip_done, 2 * s + h + 1)
                        n = nc.vector.tensor_tensor(o[:, :, h * HD:(h + 1) * HD], av[h][:, :, 0:HD],
                                                    rsum[:, h, :].unsqueeze(2).broadcast_to([P, TPG, HD]), ALU.mult)
                    n.then_inc(o_done, 1)
                    if j == 0 and not first:
                        residual(ph, G - 1)
                    if j == PAIRS - 2 and more:
                        z_split_lo(dve, G + 1, psW)
                        if ph == 1:
                            split_context(G + 1 - NGRP)

                for ph in range(2):
                    G0 = ph * NGRP
                    if ph == 0:
                        for g in range(NGRP):
                            dve.wait_ge(x_in[g], 16)
                            if g == 0:
                                ln_stats(dve, 0, 0)
                                ln_rows(dve, 0, 0)
                    else:
                        dve.wait_ge(res_done, G0)
                        ln_stats(dve, G0, 0)
                        ln_rows(dve, G0, 0)
                        split_context(0)
                    for n in range(N_ATT):
                        weights_lo(dve, ph * N_ATT + n, whole_lo[n], whole[n], CHUNK, scales[n])
                    z_split_lo(dve, G0, psW)
                    qk_split(G0, 0)
                    step(ph, G0, 0, first=True)
                    with dve.Fori(G0, G0 + NGRP - 1) as G:
                        for j in range(1, PAIRS):
                            step(ph, G, j)
                        step(ph, G + 1, 0)
                    for j in range(1, PAIRS):
                        step(ph, G0 + NGRP - 1, j, more=False)
                    oT_split((G0 + NGRP) * PAIRS)
                    residual(ph, G0 + NGRP - 1)

            @block.tensor
            def _(pe):
                pe.wait_ge(consts, 6)

                def qk_project(ph, G, j):
                    jj = j % PAIRS
                    sources = [(zhi, zlo), (chi, clo) if ph == 1 else (zhi, zlo)]
                    if jj == 0:
                        g = G + j // PAIRS
                        pe.wait_ge(z_lo, (g + 1) * KT)
                        if ph == 1:
                            pe.wait_ge(c_lo, g + 1 - NGRP)
                    if j == 1:
                        pe.wait_ge(v_done, G * 2 * TPG + TPG)
                    elif 2 <= j <= TPG + 1:
                        pe.wait_ge(v_done, G * 2 * TPG + TPG + j - 1)
                    for n, (hi, lo) in enumerate(sources):
                        for k in range(KT):
                            c = slice(jj * P, (jj + 1) * P)
                            mm = product(psW[:, n, :], (wh[n][:, k, c], wl[n][:, k, c]), (hi[:, k, :], lo[:, k, :]),
                                         k == 0, k == KT - 1)
                        mm.then_inc(qk_mm, 1)

                def v_project(ph, half, t, bank):
                    hi, lo = (chi, clo) if ph == 1 else (zhi, zlo)
                    c = slice(half * HALF * HD, (half + 1) * HALF * HD)
                    r = slice(t * P, (t + 1) * P)
                    for k in range(KT):
                        mm = product(psW[:, bank, :], (hi[:, k, r], lo[:, k, r]), (wh[V][:, k, c], wl[V][:, k, c]),
                                     k == 0, k == KT - 1)
                    mm.then_inc(v_mm, 1)

                def v_first_half(ph, G):
                    s2 = G * 2 * PAIRS
                    for t in range(TPG):
                        if t < 2:
                            pe.wait_ge(qk_lo, s2 + t + 1)
                        else:
                            pe.wait_ge(v_done, G * 2 * TPG + t - 1)
                        v_project(ph, 0, t, t % 2)

                def oT_transposes(s):
                    pe.wait_ge(o_done, s)
                    for t in range(TPG):
                        mm = nc.tensor.transpose(psT[:, 0, t * P:(t + 1) * P], o[:, t, :], ident[:])
                    mm.then_inc(oT_mm, 1)

                def out_project(s, j, tiles):
                    pe.wait_ge(oT_lo, s)
                    for t in tiles:
                        r = slice(t * P, (t + 1) * P)
                        mm = product(psA[:, t // 2, (t % 2) * D:(t % 2 + 1) * D], (othi[:, r], otlo[:, r]),
                                     (wo_hi[:, j, :], wo_lo[:, j, :]), j == 0 and t % 2 == 0, j == PAIRS - 1,
                                     skip_group_check=True)
                    if tiles[-1] == TPG - 1:
                        mm.then_inc(proj_mm, 1)

                def scores(ph, s, j):
                    pe.wait_ge(qk_lo, 2 * s + 2)
                    if ph == 0:
                        for h in range(2):
                            nc.tensor.matmul(psS[:, h, :], identb[:], maskb[:].rearrange("p a b -> p (a b)"),
                                             start=True, stop=False, skip_group_check=True)
                    q = j % 2
                    for b in range(TPG):
                        c = slice(b * P, (b + 1) * P)
                        for n, (left, right) in enumerate(((qkhi, qklo), (qkhi, qkhi), (qklo, qkhi))):
                            for h in range(2):
                                r = slice(h * HD, (h + 1) * HD)
                                mm = nc.tensor.matmul(psS[:, h, c], left[r, q, Q, c], right[r, q, K, c],
                                                      start=ph == 1 and n == 0, stop=n == 2, skip_group_check=True)
                    mm.then_inc(s_mm, 1)

                def step(ph, G, j, first=False, more=True):
                    s = G * PAIRS + j
                    if not first:
                        oT_transposes(s)
                    elif not (isinstance(s, int) and s == 0):
                        pe.wait_ge(o_done, s)
                    scores(ph, s, j)
                    if j + 1 < PAIRS or more:
                        qk_project(ph, G, j + 1)
                    if not first:
                        pe.wait_ge(oT_lo, s)
                    for h in range(2):
                        pe.wait_ge(exp_done, 2 * s + h + 1)
                        for b in range(TPG):
                            mm = nc.tensor.transpose(psT[:, h, b * P:(b + 1) * P], prob[:, h, b, :], ident[:])
                        mm.then_inc(pT_mm, 1)
                    if not first:
                        if j == 1 and not (isinstance(G, int) and G == 0):
                            pe.wait_ge(res_done, G)
                        out_project(s, (j - 1) % PAIRS, range(0, 2))
                    if j % (PAIRS // 2) == 0:
                        pe.wait_ge(v_done, G * 2 * TPG + (TPG if j == 0 else 2 * TPG))
                    for h, done in enumerate((pT0_done, pT1_done)):
                        pe.wait_ge(done, s + 1)
                        for b in range(TPG):
                            mm = nc.tensor.matmul(psS[:, h, b * VP:(b + 1) * VP], probT[:, h, b * P:(b + 1) * P],
                                                  v[:, b, 2 * j + h, :], start=True, stop=True)
                        mm.then_inc(av_mm, 1)
                    if not first:
                        out_project(s, (j - 1) % PAIRS, range(2, TPG))
                    if j < TPG:
                        pe.wait_ge(qk_lo, 2 * s + 3)
                        v_project(ph, 1, j, 0)
                    if j == PAIRS - 2 and more:
                        pe.wait_ge(qk_lo, 2 * s + 4)
                        z_transposes(pe, G + 1, psW)
                    if j == PAIRS - 1 and more:
                        v_first_half(ph, G + 1)

                for ph in range(2):
                    G0 = ph * NGRP
                    z_transposes(pe, G0, psW)
                    pe.wait_ge(w_lo, ph * N_ATT + N_ATT)
                    qk_project(ph, G0, 0)
                    v_first_half(ph, G0)
                    step(ph, G0, 0, first=True)
                    with pe.Fori(G0, G0 + NGRP - 1) as G:
                        for j in range(1, PAIRS):
                            step(ph, G, j)
                        step(ph, G + 1, 0)
                    for j in range(1, PAIRS):
                        step(ph, G0 + NGRP - 1, j, more=False)
                    end = (G0 + NGRP) * PAIRS
                    oT_transposes(end)
                    out_project(end, PAIRS - 1, range(TPG))

        ffn = ExitStack()
        with ffn:
            def fb(name, shape, dt=F32):
                return sb(name, shape, dt, ffn)

            w1s = [fb(f"w1_{n}", [P, KT, 2 * HID], F32R) for n in ("hi", "lo")]
            wins = [fb(f"win_{n}", [P, KT, 2 * HID], F32R) for n in ("hi", "lo")]
            wouts = [fb(f"wout_{n}", [P, HT, D], F32R) for n in ("hi", "lo")]
            w2s = [fb(f"w2_{n}", [P, HT, NE * D], F32R) for n in ("hi", "lo")]
            graw = fb("graw", [P, KT, NG])
            gws = [fb(f"gw_{n}", [P, KT, NG], F32R) for n in ("hi", "lo")]
            gbias = fb("gbias", [1, NG])
            ones = fb("ones", [1, P])
            earlier = fb("earlier", [P, NE, NE])
            hids = [fb(f"hid_{n}", [P, 2 * HT, GT], F32R) for n in ("hi", "lo")]
            silu = fb("silu", [P, 2, GT])
            h = fb("h", [P, 2, GT])
            logits = fb("logits", [P, TPG, NG])
            gmax = fb("gmax", [P, TPG])
            emax = fb("emax", [P, TPG, GROUPS])
            probs = fb("probs", [P, TPG, NG])
            gsum = fb("gsum", [P, TPG])
            esum = fb("esum", [P, TPG, GROUPS])
            chosen = fb("chosen", [P, TPG, GROUPS])
            coef = fb("coef", [P, TPG, GROUPS])
            above = fb("above", [P, TPG, NE, NE])
            ties = fb("ties", [P, TPG, NE, NE])
            rank = fb("rank", [P, TPG, NE])
            wse = fb("wse", [P, TPG, NE])
            acc = fb("acc", [P, 2, D])
            fin = fb("fin", [P, FIN, D])
            AB = [psS[:, 0, :], psS[:, 1, :], psW[:, 0, :], psW[:, 1, :]]
            OB = [psT[:, 0, :], psT[:, 1, :], psA[:, 0, :], psA[:, 1, :]]
            N0 = 2 * N_ATT
            L0 = 2 * NGRP
            MT = 2 * HT
            GSTEPS = 19
            parts = [(w1s, 0, KT * 2 * HID), (wins, 0, KT * 2 * HID), (wouts, 0, HT * D)] + \
                    [(w2s, k, NE * D) for k in range(HT)]

            def part(n, which):
                ws, k, size = parts[n]
                return (ws[which][:, k, :] if ws is w2s else flat(ws[which][:])), size

            block2 = ffn.enter_context(nc.Block())

            @block2.sync
            def _(sp):
                for slot in stored:
                    sp.sem_inc(slot, 16)
                sp.wait_ge(proj_mm, 2 * NGRP * PAIRS)
                sp.dma_start(graw[:], wgate.rearrange("(k p) n -> p k n", p=P)).then_inc(gate_in, 16)
                sp.dma_start(gbias[:], bgate).then_inc(gate_in, 16)
                for i in range(N_FFN):
                    n = N0 + i
                    sp.wait_ge(w_lo, n - STAGES + 1)
                    _, size = part(i, 0)
                    if i < 3:
                        src, k = pieces[n]
                        sp.dma_start(piece(n, size).rearrange("p (k n) -> p k n", k=k), src)\
                            .then_inc(stage_in[n % STAGES], 16)
                    else:
                        sp.dma_start(piece(n, size), w2_rows[i - 3]).then_inc(stage_in[n % STAGES], 16)
                with sp.Fori(0, NGRP) as g:
                    for t in range(TPG):
                        sp.wait_ge(fin_done, g * TPG + t + 1)
                        sp.dma_start(out[bass.ds((g * TPG + t) * P, P), :], fin[:, t % FIN, :]).then_inc(stored[t % FIN], 16)
                for slot in stored:
                    sp.wait_ge(slot, 16 * (B // FIN + 1))

            @block2.gpsimd
            def _(pool):
                pool.wait_ge(res_done, 2 * NGRP)
                nc.gpsimd.memset(ones[:], 1.0).then_inc(ffn_consts, 1)
                nc.gpsimd.memset(earlier[:], 1.0).then_inc(ffn_ones, 1)
                pool.wait_ge(ffn_ones, 1)
                nc.gpsimd.affine_select(out=earlier[:], in_=earlier[:], compare_op=ALU.is_gt, fill=0.0, base=0,
                                        pattern=[[1, NE], [-1, NE]], channel_multiplier=0).then_inc(ffn_consts, 1)
                ln_scale(pool, 2 * NGRP, 3 * NGRP)

            @block2.scalar
            def _(act):
                def group(g):
                    z_split_hi(act, g + L0, psS)
                    for m in range(MT):
                        act.wait_ge(ab_mm, g * MT + m + 1)
                        if not (isinstance(g, int) and g == 0 and m < 2):
                            act.wait_ge(h_done, g * MT + m - 1)
                        nc.scalar.activation(silu[:, m % 2, :], AB[2 * (m % 2)], ACT.Silu).then_inc(silu_done, 1)
                        if m >= 1:
                            split(g, m - 1)
                    split(g, MT - 1)
                    act.wait_ge(gate_step, g * GSTEPS + 4)
                    nc.scalar.activation(flat(probs[:]), flat(logits[:]), ACT.Exp).then_inc(gate_exp, 1)

                def split(g, m):
                    act.wait_ge(h_done, g * MT + m + 1)
                    nc.scalar.activation(hids[0][:, m, :], h[:, m % 2, :], ACT.Copy).then_inc(h_hi, 1)

                act.wait_ge(proj_mm, 2 * NGRP * PAIRS)
                act.wait_ge(oT_lo, 2 * NGRP * PAIRS)
                act.wait_ge(gate_in, 32)
                nc.scalar.activation(flat(gws[0][:]), flat(graw[:]), ACT.Copy).then_inc(c_hi, 1)
                for n in range(2):
                    weights_hi(act, N0 + n, *part(n, 0))
                for n in range(2, N_FFN):
                    weights_hi(act, N0 + n, *part(n, 0))
                group(0)
                with act.Fori(1, NGRP) as g:
                    group(g)

            @block2.vector
            def _(dve):
                def gating(g):
                    count = [0]

                    def link(ins):
                        count[0] += 1
                        ins.then_inc(gate_step, 1)

                    def linked():
                        dve.wait_ge(gate_step, g * GSTEPS + count[0])

                    def wide(ap, n):
                        return ap.unsqueeze(len(ap.shape)).broadcast_to([*ap.shape, n])

                    lg = logits[:, :, 0:GROUPS]
                    le = logits[:, :, GROUPS:NG].rearrange("p t (g e) -> p t g e", g=GROUPS)
                    pg = probs[:, :, 0:GROUPS]
                    pe_ = probs[:, :, GROUPS:NG]
                    pe4 = pe_.rearrange("p t (g e) -> p t g e", g=GROUPS)
                    dve.wait_ge(gate_copied, g + 1)
                    link(nc.vector.tensor_reduce(gmax[:], lg, AX.X, ALU.max))
                    link(nc.vector.tensor_reduce(emax[:], le, AX.X, ALU.max))
                    linked()
                    link(nc.vector.tensor_tensor(lg, lg, wide(gmax[:], GROUPS), ALU.subtract))
                    link(nc.vector.tensor_tensor(le, le, wide(emax[:], PER_GROUP), ALU.subtract))
                    dve.wait_ge(gate_exp, g + 1)
                    link(nc.vector.tensor_reduce(gsum[:], pg, AX.X, ALU.add))
                    link(nc.vector.tensor_reduce(esum[:], pe4, AX.X, ALU.add))
                    linked()
                    link(nc.vector.reciprocal(gsum[:], gsum[:]))
                    link(nc.vector.reciprocal(esum[:], esum[:]))
                    linked()
                    link(nc.vector.tensor_tensor(pg, pg, wide(gsum[:], GROUPS), ALU.mult))
                    linked()
                    link(nc.vector.tensor_tensor(chosen[:, :, 0], pg[:, :, 0], pg[:, :, 1], ALU.is_ge))
                    link(nc.vector.tensor_tensor(chosen[:, :, 1], pg[:, :, 0], pg[:, :, 1], ALU.is_lt))
                    linked()
                    link(nc.vector.tensor_tensor(chosen[:], chosen[:], pg, ALU.mult))
                    linked()
                    link(nc.vector.tensor_tensor(coef[:], chosen[:], esum[:], ALU.mult))
                    linked()
                    link(nc.vector.tensor_tensor(pe4, pe4, wide(coef[:], PER_GROUP), ALU.mult))
                    linked()
                    this = wide(pe_, NE)
                    other = pe_.unsqueeze(2).broadcast_to([P, TPG, NE, NE])
                    link(nc.vector.tensor_tensor(above[:], other, this, ALU.is_gt))
                    link(nc.vector.tensor_tensor(ties[:], other, this, ALU.is_equal))
                    linked()
                    link(nc.vector.tensor_tensor(ties[:], ties[:],
                                                 earlier[:].unsqueeze(1).broadcast_to([P, TPG, NE, NE]), ALU.mult))
                    linked()
                    link(nc.vector.tensor_tensor(above[:], above[:], ties[:], ALU.add))
                    linked()
                    link(nc.vector.tensor_reduce(rank[:], above[:], AX.X, ALU.add))
                    linked()
                    assert count[0] == GSTEPS
                    nc.vector.scalar_tensor_tensor(wse[:], rank[:], TOP_K - 0.5, pe_, ALU.is_lt,
                                                   ALU.mult).then_inc(wse_done, 1)
                    dve.wait_ge(wse_done, g + 1)

                def hidden(g):
                    dve.wait_ge(gate_mm, g + 1)
                    nc.vector.tensor_copy(flat(logits[:]), AB[2][:, 0:TPG * NG]).then_inc(gate_copied, 1)
                    for m in range(MT):
                        dve.wait_ge(silu_done, g * MT + m + 1)
                        if not (isinstance(g, int) and g == 0 and m < 2):
                            dve.wait_ge(h_lo, g * MT + m - 1)
                        nc.vector.tensor_tensor(h[:, m % 2, :], AB[2 * (m % 2) + 1], silu[:, m % 2, :],
                                                ALU.mult).then_inc(h_done, 1)
                        if m >= 1:
                            split(g, m - 1)
                    split(g, MT - 1)

                def split(g, m):
                    dve.wait_ge(h_hi, g * MT + m + 1)
                    nc.vector.tensor_tensor(hids[1][:, m, :], h[:, m % 2, :], hids[0][:, m, :].bitcast(F32),
                                            ALU.subtract).then_inc(h_lo, 1)

                def combine(g, t):
                    n0, a0 = g * TPG * OUTS + t * OUTS, (g * TPG + t + 1) * NE
                    chains = [fin[:, t % FIN, :], acc[:, t % 2, :]]
                    for c in range(OUTS - 1):
                        dve.wait_ge(out_mm, n0 + c + 1)
                        for i in range(2):
                            e = 2 * c + i
                            src, w, dst = OB[(t * OUTS + c) % 4][:, i * D:(i + 1) * D], wse[:, t, e:e + 1], chains[i]
                            if c:
                                dve.wait_ge(acc_done, a0 + e - 1)
                            if c == 0 and i == 0:
                                dve.wait_ge(stored[t % FIN], (g * (TPG // FIN) + t // FIN + 1) * 16)
                                ins = nc.vector.scalar_tensor_tensor(dst, src, w, row_tile(g, t), ALU.mult, ALU.add)
                            elif c == 0:
                                ins = nc.vector.tensor_scalar(dst, src, w, None, ALU.mult)
                            else:
                                ins = nc.vector.scalar_tensor_tensor(dst, src, w, dst, ALU.mult, ALU.add)
                            ins.then_inc(acc_done, 1)
                    dve.wait_ge(out_mm, n0 + OUTS)
                    dve.wait_ge(acc_done, a0 + NE)
                    nc.vector.tensor_tensor(chains[1], OB[(t * OUTS + OUTS - 1) % 4][:, 0:D], chains[1],
                                            ALU.add).then_inc(out_used, 1)
                    dve.wait_ge(out_used, g * TPG + t + 2)
                    nc.vector.tensor_tensor(chains[0], chains[0], chains[1], ALU.add).then_inc(fin_done, 1)

                def outputs(g, more=True):
                    if more:
                        ln_stats(dve, g + 1 + L0, g + 1)
                    combine(g, 0)
                    if more:
                        ln_rows(dve, g + 1 + L0, g + 1)
                    combine(g, 1)
                    combine(g, 2)
                    combine(g, 3)
                    if more:
                        z_split_lo(dve, g + 1 + L0, psS)

                dve.sem_inc(acc_done, NE)
                dve.sem_inc(out_used, 1)
                dve.wait_ge(res_done, L0)
                dve.wait_ge(proj_mm, 2 * NGRP * PAIRS)
                ln_stats(dve, L0, 0)
                ln_rows(dve, L0, 0)
                dve.wait_ge(c_hi, NGRP + 1)
                nc.vector.tensor_tensor(flat(gws[1][:]), flat(graw[:]), flat(gws[0][:]).bitcast(F32),
                                        ALU.subtract).then_inc(c_lo, 1)
                for n in range(N_FFN):
                    dst, size = part(n, 1)
                    weights_lo(dve, N0 + n, dst, part(n, 0)[0], size)
                z_split_lo(dve, L0, psS)
                dve.wait_ge(ffn_consts, 2)
                hidden(0)
                gating(0)
                with dve.Fori(0, NGRP - 1) as g:
                    outputs(g)
                    hidden(g + 1)
                    gating(g + 1)
                outputs(NGRP - 1, more=False)

            @block2.tensor
            def _(pe):
                def hidden(g):
                    pe.wait_ge(z_lo, (g + L0 + 1) * KT)
                    for t in range(TPG):
                        r = slice(t * P, (t + 1) * P)
                        dst = AB[2][:, t * NG:(t + 1) * NG]
                        nc.tensor.matmul(dst, ones[:], gbias[:], start=True, stop=False)
                        for k in range(KT):
                            mm = product(dst, (zhi[:, k, r], zlo[:, k, r]), (gws[0][:, k, :], gws[1][:, k, :]),
                                         False, k == KT - 1)
                    mm.then_inc(gate_mm, 1)
                    for m in range(MT):
                        ws = w1s if m < HT else wins
                        if m == 1:
                            pe.wait_ge(gate_copied, g + 1)
                        if m >= 2:
                            pe.wait_ge(h_done, g * MT + m - 1)
                        for half in range(2):
                            c = slice(half * HID + (m % HT) * P, half * HID + (m % HT + 1) * P)
                            for k in range(KT):
                                mm = product(AB[2 * (m % 2) + half], (ws[0][:, k, c], ws[1][:, k, c]),
                                             (zhi[:, k, :], zlo[:, k, :]), k == 0, k == KT - 1)
                        mm.then_inc(ab_mm, 1)

                def outputs(g, more=True):
                    for t in range(TPG):
                        r = slice(t * P, (t + 1) * P)
                        for c in range(OUTS):
                            n = t * OUTS + c
                            shared = c == OUTS - 1
                            if t == 0:
                                if c == 0:
                                    pe.wait_ge(h_lo, g * MT + HT)
                                if shared:
                                    pe.wait_ge(h_lo, g * MT + MT)
                            back, place = (n - 4) // OUTS, (n - 4) % OUTS
                            if place == OUTS - 1:
                                pe.wait_ge(out_used, g * TPG + back + 2)
                            else:
                                pe.wait_ge(acc_done, (g * TPG + back + 1) * NE + 2 * place + 2)
                            for k in range(HT):
                                m = HT + k if shared else k
                                lhs = (hids[0][:, m, r], hids[1][:, m, r])
                                cols_ = slice(c * 2 * D, (c + 1) * 2 * D)
                                rhs = tuple(w[:, k, :] for w in wouts) if shared else tuple(w[:, k, cols_] for w in w2s)
                                dst = OB[n % 4][:, 0:D] if shared else OB[n % 4]
                                mm = product(dst, lhs, rhs, k == 0, k == HT - 1)
                            mm.then_inc(out_mm, 1)
                        if t == 2 and more:
                            pe.wait_ge(h_done, (g + 1) * MT)
                            z_transposes(pe, g + 1 + L0, psS)

                pe.wait_ge(res_done, L0)
                z_transposes(pe, L0, psS)
                pe.wait_ge(ffn_consts, 2)
                pe.wait_ge(gate_in, 32)
                pe.wait_ge(c_lo, NGRP + 1)
                pe.wait_ge(w_lo, N0 + N_FFN)
                hidden(0)
                with pe.Fori(0, NGRP - 1) as g:
                    outputs(g)
                    hidden(g + 1)
                outputs(NGRP - 1, more=False)


def kernel(**inputs):
    import numpy as _np
    import concourse.bacc as _bacc
    from concourse import mybir as _mybir
    from concourse.bass_utils import run_bass_kernel_spmd as _run

    def c(a):
        return _np.ascontiguousarray(a)

    a = {k: _np.asarray(v) for k, v in inputs.items()}
    tokens = a["x"].shape[0] * a["x"].shape[1]
    d = a["x"].shape[2]
    w2 = a["L0_ffn_w2"]
    arrays = {
        "x": c(a["x"].reshape(tokens, d)),
        "ctxT": c(a["ctx_1024"].reshape(tokens, d).T),
        "wq": c(a["L0_attn_Wq"]), "wk": c(a["L0_attn_Wk"]), "wv": c(a["L0_attn_Wv"]), "wr": c(a["L0_attn_Wr"]),
        "xq": c(a["L0_xattn_w_q"]), "xk": c(a["L0_xattn_w_k"]), "xv": c(a["L0_xattn_w_v"]), "xr": c(a["L0_xattn_w_o"]),
        "w1": c(a["L0_ffn_w1"].T), "win": c(a["L0_ffn_w_in"].T), "wout": c(a["L0_ffn_w_out"].T),
        "w2": c(w2.transpose(2, 0, 1).reshape(w2.shape[2], w2.shape[0] * w2.shape[1])),
        "wgate": c(_np.concatenate([a["L0_ffn_wg"], a["L0_ffn_we"]], 0).T),
        "bgate": c(_np.concatenate([a["L0_ffn_gb"], a["L0_ffn_eb"]])[None, :]),
    }
    nc = _bacc.Bacc("TRN2", target_bir_lowering=False, num_devices=1)
    args = [nc.dram_tensor(n, v.shape, _mybir.dt.from_np(v.dtype), kind="ExternalInput").ap() for n, v in arrays.items()]
    out = nc.dram_tensor("out", (tokens, d), _mybir.dt.float32, kind="ExternalOutput").ap()
    build(nc, *args, out)
    r = _run(nc, [arrays], core_ids=[0])
    return r.results[0]["out"].reshape(a["x"].shape)
```

```python
from contextlib import ExitStack

import concourse.bass as bass
from concourse import mybir

F32 = mybir.dt.float32
F32R = mybir.dt.float32r
BF16 = mybir.dt.bfloat16
ACT = mybir.ActivationFunctionType
ALU = mybir.AluOpType
AX = mybir.AxisListType

P = 128
B, S, D = 16, 128, 256
HEADS, HD = 16, 64
INNER = HEADS * HD
HID = 512
GROUPS, PER_GROUP = 2, 4
NE = GROUPS * PER_GROUP
NG = GROUPS + NE
TOP_K = 2
EPS = 1e-5
MASK = -50.0
SCALE = HD ** -0.5

TPG = 4
GT = TPG * P
NGRP = B // TPG
KT = D // P
PAIRS = HEADS // 2
HT = HID // P
HALF = HEADS // 2
CHUNK = KT * INNER
STAGES = 3
FIN = 2
OUTS = NE // 2 + 1


def build(nc, x, ctxT, wq, wk, wv, wr, xq, xk, xv, xr, w1, win, wout, w2, wgate, bgate, out):
    ctx = ExitStack()
    with ctx:
        def sem(name):
            return ctx.enter_context(nc.semaphore(name))

        def sb(name, shape, dt=F32, stack=ctx):
            return stack.enter_context(nc.sbuf_tensor(name, shape, dt))

        def ps(name):
            return ctx.enter_context(nc.psum_tensor(name, [P, 2, 512], F32))

        xres = sb("xres", [P, B, D])
        stage = sb("stage", [P, STAGES, CHUNK])
        ident = sb("ident", [P, P])
        identb = sb("identb", [P, P], BF16)
        maskb = sb("maskb", [P, TPG, P], BF16)
        z = sb("z", [P, TPG, D])
        zhi = sb("zhi", [P, KT, GT], F32R)
        zlo = sb("zlo", [P, KT, GT], F32R)
        bnst = sb("bnst", [P, TPG, 6])
        mv = sb("mv", [P, TPG, 2])
        veps = sb("veps", [P, TPG])
        rstd = sb("rstd", [P, TPG])
        mhalf = sb("mhalf", [P, TPG])
        eps = sb("eps", [P, TPG])
        psS, psW, psT, psA = ps("psS"), ps("psW"), ps("psT"), ps("psA")

        x_in = [sem(f"x_in{g}") for g in range(NGRP)]
        stage_in = [sem(f"stage_in{k}") for k in range(STAGES)]
        gate_in, ctx_in = sem("gate_in"), sem("ctx_in")
        zeroed, consts, ffn_ones, ffn_consts = sem("zeroed"), sem("consts"), sem("ffn_ones"), sem("ffn_consts")
        w_hi, w_lo = sem("w_hi"), sem("w_lo")
        g_hi, g_lo = sem("g_hi"), sem("g_lo")
        c_hi, c_lo = sem("c_hi"), sem("c_lo")
        bn_done, bn_seen, mv_done, eps_done, rstd_done, z_done = (
            sem("bn_done"), sem("bn_seen"), sem("mv_done"), sem("eps_done"), sem("rstd_done"), sem("z_done"))
        zT_mm, z_hi, z_lo = sem("zT_mm"), sem("z_hi"), sem("z_lo")
        qk_mm, q_hi, q_lo, k_hi, k_lo = sem("qk_mm"), sem("q_hi"), sem("q_lo"), sem("k_hi"), sem("k_lo")
        v_mm, v_hi, v_lo = sem("v_mm"), sem("v_hi"), sem("v_lo")
        s_mm, max_done, exp_done, recip_done, prob_done = (
            sem("s_mm"), sem("max_done"), sem("exp_done"), sem("recip_done"), sem("prob_done"))
        pT_mm, pT_hi, pT_lo = sem("pT_mm"), sem("pT_hi"), sem("pT_lo")
        oT_mm, oT_hi, oT_lo = sem("oT_mm"), sem("oT_hi"), sem("oT_lo")
        proj_mm, res_done = sem("proj_mm"), sem("res_done")
        gate_mm, gate_biased, gate_T, gate_copied, gate_step, gate_exp, wse_done = (
            sem("gate_mm"), sem("gate_biased"), sem("gate_T"), sem("gate_copied"), sem("gate_step"), sem("gate_exp"), sem("wse_done"))
        ab_mm, silu_done, h_done, h_hi, h_lo = (
            sem("ab_mm"), sem("silu_done"), sem("h_done"), sem("h_hi"), sem("h_lo"))
        out_mm, out_used, acc_done, fin_done = sem("out_mm"), sem("out_used"), sem("acc_done"), sem("fin_done")
        stored = [sem(f"stored{i}") for i in range(FIN)]

        def flat(ap):
            return ap.rearrange("p a b -> p (a b)")

        def rows(g):
            return xres[:, bass.ds(g * TPG, TPG), :]

        def row_tile(g, t):
            return flat(xres[:, bass.ds(g * TPG + t, 1), :])

        def product(o, lhs, rhs, start, stop, **kw):
            (lh, ll), (rh, rl) = lhs, rhs
            nc.tensor.matmul(o, lh, rl, start=start, stop=False, **kw)
            nc.tensor.matmul(o, lh, rh, start=False, stop=False, **kw)
            return nc.tensor.matmul(o, ll, rh, start=False, stop=stop, **kw)

        def ln_stats(dve, g, row_g):
            for t in range(TPG):
                nc.vector.bn_stats(bnst[:, t, :], row_tile(row_g, t)).then_inc(bn_done, 1)
            dve.wait_ge(bn_done, (g + 1) * TPG)
            dve.sem_inc(bn_seen, 1)
            for t in range(TPG):
                nc.vector.bn_aggr(mv[:, t, :], bnst[:, t, :]).then_inc(mv_done, 1)

        def ln_rows(dve, g, row_g):
            dve.wait_ge(rstd_done, g + 1)
            if not (isinstance(g, int) and g == 0):
                dve.wait_ge(zT_mm, g * KT)
            for t in range(TPG):
                nc.vector.tensor_scalar(z[:, t, :], row_tile(row_g, t), mv[:, t, 0:1], rstd[:, t:t + 1],
                                        ALU.subtract, ALU.mult).then_inc(z_done, 1)

        def ln_scale(pool, g):
            pool.wait_ge(mv_done, (g + 1) * TPG)
            nc.gpsimd.tensor_tensor(veps[:], mv[:, :, 1], eps[:], ALU.add).then_inc(eps_done, 1)
            pool.wait_ge(eps_done, g + 1)
            nc.gpsimd.tensor_tensor(rstd[:], veps[:], mhalf[:], ALU.pow).then_inc(rstd_done, 1)

        def z_transposes(pe, g, banks):
            pe.wait_ge(z_done, (g + 1) * TPG)
            for k in range(KT):
                for t in range(TPG):
                    mm = nc.tensor.transpose(banks[:, k, t * P:(t + 1) * P], z[:, t, k * P:(k + 1) * P], ident[:])
                mm.then_inc(zT_mm, 1)

        def z_split_hi(act, g, banks):
            for k in range(KT):
                act.wait_ge(zT_mm, g * KT + k + 1)
                nc.scalar.activation(zhi[:, k, :], banks[:, k, :], ACT.Copy).then_inc(z_hi, 1)

        def z_split_lo(dve, g, banks):
            for k in range(KT):
                dve.wait_ge(z_hi, g * KT + k + 1)
                nc.vector.tensor_tensor(zlo[:, k, :], banks[:, k, :], zhi[:, k, :].bitcast(F32),
                                        ALU.subtract).then_inc(z_lo, 1)

        w1s = [sb(f"w1_{n}", [P, KT, 2 * HID], F32R) for n in ("hi", "lo")]
        graw = sb("graw", [P, KT, NG])
        gbias = sb("gbias", [NG, 1])
        gws = [sb(f"gw_{n}", [P, KT, NG], F32R) for n in ("hi", "lo")]

        def piece(n, shape):
            return stage[:, n % STAGES, 0:shape[1] * shape[2]].rearrange("p (a b) -> p a b", a=shape[1])

        def load(sp, n, src):
            if n >= STAGES:
                sp.wait_ge(w_lo, n - STAGES + 1)
            sp.dma_start(piece(n, src.shape), src).then_inc(stage_in[n % STAGES], 16)

        def weights_hi(act, n, dst, scale=1.0):
            act.wait_ge(stage_in[n % STAGES], 16 * (n // STAGES + 1))
            nc.scalar.activation(dst, piece(n, dst.shape), ACT.Copy, scale=scale).then_inc(w_hi, 1)

        def weights_lo(dve, n, dst, hi, scale=1.0):
            dve.wait_ge(w_hi, n + 1)
            nc.vector.scalar_tensor_tensor(dst, piece(n, dst.shape), scale, hi.bitcast(F32),
                                           ALU.mult, ALU.subtract).then_inc(w_lo, 1)

        def k_rows(w):
            return w.rearrange("(k p) n -> p k n", p=P)

        w2_rows = w2.rearrange("(k p) (e n) -> k p e n", p=P, e=NE)

        att = ExitStack()
        with att:
            def ab(name, shape, dt=F32):
                return sb(name, shape, dt, att)

            wh = [ab(f"w{n}_hi", [P, KT, INNER], F32R) for n in "qkv"]
            wl = [ab(f"w{n}_lo", [P, KT, INNER], F32R) for n in "qkv"]
            wo_hi = ab("wo_hi", [P, PAIRS, D], F32R)
            wo_lo = ab("wo_lo", [P, PAIRS, D], F32R)
            craw = stage[:, 2, CHUNK // 2:].rearrange("p (k t) -> p k t", k=KT)
            chi = ab("chi", [P, KT, GT], F32R)
            clo = ab("clo", [P, KT, GT], F32R)
            q = [ab(f"q_{n}", [P, GT], F32R) for n in ("hi", "lo")]
            kd = [ab(f"kd_{n}", [P, TPG, 2, P], F32R) for n in ("hi", "lo")]
            v = [ab(f"v_{n}", [P, TPG, INNER], F32R) for n in ("hi", "lo")]
            nmax = ab("nmax", [P, TPG * 2])
            prob = ab("prob", [P, TPG * 2, P])
            psum_ = ab("psum", [P, TPG * 2])
            rsum = ab("rsum", [P, TPG * 2])
            pT = [ab(f"pT_{n}", [P, 2, GT], F32R) for n in ("hi", "lo")]
            oT = [ab(f"oT_{n}", [P, 2, TPG, P], F32R) for n in ("hi", "lo")]
            Q, K, V = 0, 1, 2
            HC, HP = INNER // 2, PAIRS // 2
            lower, upper = slice(0, HC), slice(HC, INNER)

            pieces = [(k_rows(w), h[:], l[:], f) for w, h, l, f in
                      ((wq, wh[Q], wl[Q], SCALE), (wk, wh[K], wl[K], 1.0), (wv, wh[V], wl[V], 1.0), (wr, wo_hi, wo_lo, 1.0))]
            N_SELF = len(pieces)
            pieces += [(k_rows(xv), wh[V][:], wl[V][:], 1.0)]
            for c, r in ((lower, slice(0, HP)), (upper, slice(HP, PAIRS))):
                pieces += [(k_rows(xq)[:, :, c], wh[Q][:, :, c], wl[Q][:, :, c], SCALE),
                           (k_rows(xk)[:, :, c], wh[K][:, :, c], wl[K][:, :, c], 1.0),
                           (k_rows(xr)[:, r, :], wo_hi[:, r, :], wo_lo[:, r, :], 1.0)]
            N_ATT = len(pieces)
            pieces += [(k_rows(w1), w1s[0][:], w1s[1][:], 1.0)]
            late_sources = [k_rows(win)] + [w2_rows[k] for k in range(HT)] + [k_rows(wout)]
            SWAPS = {(NGRP - 1, 4): (4,), (NGRP - 1, 5): (5, 6), (NGRP - 1, 6): (7,), (NGRP, 0): (8, 9), (NGRP, 1): (10,),
                     (2 * NGRP - 1, 3): (11,)}
            assert len(pieces) == 12
            STEPS = 2 * NGRP * PAIRS
            GATE_AT = (2 * NGRP - 1, 4)
            N_CONST = 7
            heads_ = [slice(h * HD, (h + 1) * HD) for h in range(2)]

            def banks(ps_):
                return flat(ps_[:]).rearrange("p (b h q) -> p b h q", b=TPG, h=2)

            def swaps(G, j):
                return SWAPS.get((G, j), ()) if isinstance(G, int) else ()

            block = att.enter_context(nc.Block())

            @block.sync
            def _(sp):
                xv_ = x.rearrange("(g t p) d -> g p t d", p=P, t=TPG)
                sp.dma_start(xres[:, 0:TPG, :], xv_[0]).then_inc(x_in[0], 16)

                for n in range(3):
                    load(sp, n, pieces[n][0])
                for g in range(1, NGRP):
                    sp.dma_start(xres[:, g * TPG:(g + 1) * TPG, :], xv_[g]).then_inc(x_in[g], 16)
                ctx_v = ctxT.rearrange("(k p) t -> p k t", p=P)
                sp.dma_start(graw[:], k_rows(wgate)).then_inc(gate_in, 16)
                sp.dma_start(gbias[:], bgate).then_inc(gate_in, 16)
                load(sp, 3, pieces[3][0])
                sp.wait_ge(w_lo, 3)
                sp.dma_start(craw, ctx_v[:, :, 0:GT]).then_inc(ctx_in, 16)
                for n in range(4, N_ATT):
                    load(sp, n, pieces[n][0])
                for g in range(1, NGRP):
                    sp.wait_ge(c_lo, g)
                    sp.dma_start(craw, ctx_v[:, :, g * GT:(g + 1) * GT]).then_inc(ctx_in, 16)
                sp.wait_ge(c_lo, NGRP)
                for n in range(N_ATT, len(pieces)):
                    load(sp, n, pieces[n][0])
                for i in range(STAGES):
                    load(sp, len(pieces) + i, late_sources[i])

            @block.gpsimd
            def _(pool):
                nc.gpsimd.memset(ident[:], 0.0).then_inc(zeroed, 1)
                nc.gpsimd.memset(identb[:], 0.0).then_inc(zeroed, 1)
                nc.gpsimd.memset(maskb[:], 0.0).then_inc(zeroed, 1)
                nc.gpsimd.memset(mhalf[:], -0.5).then_inc(consts, 1)
                nc.gpsimd.memset(eps[:], EPS).then_inc(consts, 1)
                for t in kd:
                    nc.gpsimd.memset(t[:].bitcast(F32), 0.0).then_inc(consts, 1)
                pool.wait_ge(zeroed, 3)
                for m in (ident, identb):
                    nc.gpsimd.affine_select(out=m[:], in_=m[:], compare_op=ALU.not_equal, fill=1.0, base=0,
                                            pattern=[[-1, P]], channel_multiplier=1).then_inc(consts, 1)
                nc.gpsimd.affine_select(out=maskb[:], in_=maskb[:], compare_op=ALU.is_ge, fill=MASK, base=0,
                                        pattern=[[0, TPG], [-1, P]], channel_multiplier=1).then_inc(consts, 1)
                pool.wait_ge(consts, N_CONST)

                def step(G, j, after):
                    s = G * PAIRS + j
                    for i in range(2):
                        pool.wait_ge(recip_done, 2 * s + i + 1)
                        r = slice(i * TPG, (i + 1) * TPG)
                        nc.gpsimd.tensor_tensor(prob[:, r, :], prob[:, r, :],
                                                rsum[:, r].unsqueeze(2).broadcast_to([P, TPG, P]),
                                                ALU.mult).then_inc(prob_done, 1)
                    if j == 2:
                        ln_scale(pool, G + 1)

                ln_scale(pool, 0)
                with pool.Fori(0, 2 * NGRP) as G:
                    for j in range(PAIRS):
                        step(G, j, 0)

            @block.scalar
            def _(act):
                act.preload_act_table(ACT.Exp)

                def split_context(cg):
                    act.wait_ge(ctx_in, (cg + 1) * 16)
                    nc.scalar.activation(flat(chi[:]), flat(craw), ACT.Copy).then_inc(c_hi, 1)

                def qk_split(G, j):
                    n = G * PAIRS + j
                    act.wait_ge(qk_mm, 2 * n + 1)
                    nc.scalar.activation(q[0][:], psW[:, Q, :], ACT.Copy).then_inc(q_hi, 1)
                    act.wait_ge(qk_mm, 2 * n + 2)
                    for h, r in enumerate(heads_):
                        nc.scalar.activation(kd[0][r, :, h, :], psW[r, K, :].rearrange("p (b k) -> p b k", b=TPG),
                                             ACT.Copy).then_inc(k_hi, 1)

                def v_split(G, half, t, bank):
                    act.wait_ge(v_mm, G * 2 * TPG + half * TPG + t + 1)
                    nc.scalar.activation(v[0][:, t, half * HC:(half + 1) * HC], psW[:, bank, :], ACT.Copy).then_inc(v_hi, 1)

                def pT_split(s):
                    for i in range(2):
                        act.wait_ge(pT_mm, 2 * s + i - 1)
                        nc.scalar.activation(pT[0][:, i, :], psT[:, i, :], ACT.Copy).then_inc(pT_hi, 1)

                def oT_split(s, parity):
                    act.wait_ge(oT_mm, s)
                    for h, r in enumerate(heads_):
                        nc.scalar.activation(oT[0][r, parity, :, :], banks(psT)[r, :, h, :], ACT.Copy).then_inc(oT_hi, 1)

                def step(G, j, after, first=False):
                    s = G * PAIRS + j
                    if not first:
                        pT_split(s)
                    for i in range(2):
                        act.wait_ge(max_done, 2 * s + i + 1)
                        if not first:
                            act.wait_ge(pT_mm, 2 * s + i - 1)
                        for n in range(i * TPG, (i + 1) * TPG):
                            e = nc.scalar.activation(prob[:, n, :], flat(psS[:])[:, n * P:(n + 1) * P], ACT.Exp,
                                                     bias=nmax[:, n:n + 1], accum_out=psum_[:, n:n + 1])
                        e.then_inc(exp_done, 1)
                    if j + 1 < PAIRS or after < 2:
                        qk_split(G, j + 1)
                    if not first:
                        oT_split(s, (j + 1) % 2)
                    if j < TPG:
                        v_split(G, 1, j, 0)
                    if j == PAIRS - 2:
                        z_split_hi(act, G + 1, psW)
                        if after == 1:
                            split_context(G + 1 - NGRP)
                    if j == PAIRS - 1 and after < 2:
                        for t in range(TPG):
                            v_split(G + 1, 0, t, t % 2)
                    for n in swaps(G, j):
                        if n == N_ATT - 1:
                            act.wait_ge(proj_mm, NGRP * PAIRS)
                        _, hi, _, scale = pieces[n]
                        weights_hi(act, n, hi, scale)
                    if isinstance(G, int) and (G, j) == GATE_AT:
                        act.wait_ge(gate_in, 32)
                        nc.scalar.activation(gws[0][:], graw[:], ACT.Copy).then_inc(g_hi, 1)

                def first_hi(n):
                    weights_hi(act, n, pieces[n][1], pieces[n][3])

                first_hi(Q)
                z_split_hi(act, 0, psW)
                first_hi(K)
                first_hi(V)
                qk_split(0, 0)
                first_hi(N_SELF - 1)
                for t in range(TPG):
                    v_split(0, 0, t, t % 2)
                step(0, 0, 0, first=True)
                step(0, 1, 0)
                with act.Fori(0, NGRP - 1) as G:
                    for j in range(2, PAIRS):
                        step(G, j, 0)
                    for j in range(2):
                        step(G + 1, j, 0)
                for j in range(2, PAIRS):
                    step(NGRP - 1, j, 1)
                for j in range(2):
                    step(NGRP, j, 1)
                with act.Fori(NGRP, 2 * NGRP - 1) as G:
                    for j in range(2, PAIRS):
                        step(G, j, 1)
                    for j in range(2):
                        step(G + 1, j, 1)
                for j in range(2, PAIRS):
                    step(2 * NGRP - 1, j, 2)
                pT_split(STEPS)
                oT_split(STEPS, 1)

            @block.vector
            def _(dve):
                def qk_split(G, j):
                    n = G * PAIRS + j
                    dve.wait_ge(q_hi, n + 1)
                    nc.vector.tensor_tensor(q[1][:], psW[:, Q, :], q[0][:].bitcast(F32), ALU.subtract).then_inc(q_lo, 1)
                    for h, r in enumerate(heads_):
                        dve.wait_ge(k_hi, 2 * n + h + 1)
                        nc.vector.tensor_tensor(kd[1][r, :, h, :], psW[r, K, :].rearrange("p (b k) -> p b k", b=TPG),
                                                kd[0][r, :, h, :].bitcast(F32), ALU.subtract).then_inc(k_lo, 1)

                def v_split(G, half, t, bank):
                    dve.wait_ge(v_hi, G * 2 * TPG + half * TPG + t + 1)
                    c = slice(half * HC, (half + 1) * HC)
                    nc.vector.tensor_tensor(v[1][:, t, c], psW[:, bank, :], v[0][:, t, c].bitcast(F32),
                                            ALU.subtract).then_inc(v_lo, 1)

                def pT_split(s):
                    for i in range(2):
                        dve.wait_ge(pT_hi, 2 * s + i - 1)
                        nc.vector.tensor_tensor(pT[1][:, i, :], psT[:, i, :], pT[0][:, i, :].bitcast(F32),
                                                ALU.subtract).then_inc(pT_lo, 1)

                def oT_split(s, parity):
                    for h, r in enumerate(heads_):
                        dve.wait_ge(oT_hi, 2 * s + h - 1)
                        nc.vector.tensor_tensor(oT[1][r, parity, :, :], banks(psT)[r, :, h, :],
                                                oT[0][r, parity, :, :].bitcast(F32), ALU.subtract).then_inc(oT_lo, 1)

                def split_context(cg):
                    dve.wait_ge(c_hi, cg + 1)
                    nc.vector.tensor_tensor(flat(clo[:]), flat(craw), flat(chi[:]).bitcast(F32),
                                            ALU.subtract).then_inc(c_lo, 1)

                def residual(G, sub):
                    dve.wait_ge(proj_mm, (G + 1) * PAIRS)
                    for i in range(2):
                        half = flat(xres[:, bass.ds((G - sub * NGRP) * TPG + 2 * i, 2), :])
                        r = nc.vector.tensor_tensor(half, psA[:, i, :], half, ALU.add)
                    r.then_inc(res_done, 1)

                def step(G, j, after, first=False, sub=0):
                    s = G * PAIRS + j
                    row_g = G + 1 - after * NGRP
                    for i in range(2):
                        dve.wait_ge(s_mm, 2 * s + i + 1)
                        nc.vector.tensor_reduce(nmax[:, i * TPG:(i + 1) * TPG], psS[:, i, :].rearrange("p (n k) -> p n k", k=P),
                                                AX.X, ALU.max, negate=True).then_inc(max_done, 1)
                    if not first:
                        pT_split(s)
                    if j == 2:
                        if after:
                            dve.wait_ge(res_done, (G + 2 - NGRP if isinstance(G, int) else NGRP) + 1)
                        ln_stats(dve, G + 1, row_g)
                    for i in range(2):
                        dve.wait_ge(exp_done, 2 * s + i + 1)
                        r = slice(i * TPG, (i + 1) * TPG)
                        nc.vector.reciprocal(rsum[:, r], psum_[:, r]).then_inc(recip_done, 1)
                    if j + 1 < PAIRS or after < 2:
                        qk_split(G, j + 1)
                    if j == 4:
                        ln_rows(dve, G + 1, row_g)
                    if not first:
                        oT_split(s, (j + 1) % 2)
                    if j == 1 and not (isinstance(G, int) and G == 0):
                        residual(G - 1, sub)
                    if j < TPG:
                        v_split(G, 1, j, 0)
                    if j == PAIRS - 2:
                        z_split_lo(dve, G + 1, psW)
                        if after == 1:
                            split_context(G + 1 - NGRP)
                    if j == PAIRS - 1 and after < 2:
                        for t in range(TPG):
                            v_split(G + 1, 0, t, t % 2)
                    for n in swaps(G, j):
                        _, hi, lo, scale = pieces[n]
                        weights_lo(dve, n, lo, hi, scale)
                    if isinstance(G, int) and (G, j) == GATE_AT:
                        dve.wait_ge(g_hi, 1)
                        nc.vector.tensor_tensor(gws[1][:], graw[:], gws[0][:].bitcast(F32),
                                                ALU.subtract).then_inc(g_lo, 1)

                def first_lo(n):
                    weights_lo(dve, n, pieces[n][2], pieces[n][1], pieces[n][3])

                dve.sem_inc(res_done, 1)
                dve.wait_ge(x_in[0], 16)
                ln_stats(dve, 0, 0)
                ln_rows(dve, 0, 0)
                first_lo(Q)
                z_split_lo(dve, 0, psW)
                first_lo(K)
                first_lo(V)
                qk_split(0, 0)
                first_lo(N_SELF - 1)
                for t in range(TPG):
                    v_split(0, 0, t, t % 2)
                for g in range(1, NGRP):
                    dve.wait_ge(x_in[g], 16)
                step(0, 0, 0, first=True)
                step(0, 1, 0)
                with dve.Fori(0, NGRP - 1) as G:
                    for j in range(2, PAIRS):
                        step(G, j, 0)
                    for j in range(2):
                        step(G + 1, j, 0)
                for j in range(2, PAIRS):
                    step(NGRP - 1, j, 1)
                for j in range(2):
                    step(NGRP, j, 1)
                with dve.Fori(NGRP, 2 * NGRP - 1) as G:
                    for j in range(2, PAIRS):
                        step(G, j, 1)
                    for j in range(2):
                        step(G + 1, j, 1, sub=1)
                for j in range(2, PAIRS):
                    step(2 * NGRP - 1, j, 2)
                pT_split(STEPS)
                oT_split(STEPS, 1)
                residual(2 * NGRP - 1, 1)

            @block.tensor
            def _(pe):
                pe.wait_ge(consts, N_CONST)

                def qk_project(sub, G, j):
                    jj = j % PAIRS
                    sources = [(zhi, zlo), (chi, clo) if sub == 1 else (zhi, zlo)]
                    if jj == 0:
                        g = G + j // PAIRS
                        pe.wait_ge(z_lo, (g + 1) * KT)
                        if sub == 1:
                            pe.wait_ge(c_lo, g + 1 - NGRP)
                    if jj % HP == 0:
                        pe.wait_ge(w_lo, (7 if jj == 0 else 10) if sub == 1 else 2)
                    if j == 1:
                        pe.wait_ge(v_lo, G * 2 * TPG + TPG)
                    elif 2 <= j <= TPG + 1:
                        pe.wait_ge(v_lo, G * 2 * TPG + TPG + j - 1)
                    for n, (hi, lo) in enumerate(sources):
                        for k in range(KT):
                            c = slice(jj * P, (jj + 1) * P)
                            mm = product(psW[:, n, :], (wh[n][:, k, c], wl[n][:, k, c]), (hi[:, k, :], lo[:, k, :]),
                                         k == 0, k == KT - 1)
                        mm.then_inc(qk_mm, 1)

                def v_project(sub, half, t, bank):
                    hi, lo = (chi, clo) if sub == 1 else (zhi, zlo)
                    c = slice(half * HALF * HD, (half + 1) * HALF * HD)
                    r = slice(t * P, (t + 1) * P)
                    for k in range(KT):
                        mm = product(psW[:, bank, :], (hi[:, k, r], lo[:, k, r]), (wh[V][:, k, c], wl[V][:, k, c]),
                                     k == 0, k == KT - 1)
                    mm.then_inc(v_mm, 1)

                def v_first_half(sub, G):
                    for t in range(TPG):
                        if t < 2:
                            pe.wait_ge((q_lo, k_lo)[t], (t + 1) * (G * PAIRS + 1))
                        else:
                            pe.wait_ge(v_lo, G * 2 * TPG + t - 1)
                        v_project(sub, 0, t, t % 2)

                def scores(sub, s, first=False):
                    pe.wait_ge(q_lo, s + 1)
                    pe.wait_ge(k_lo, 2 * s + 2)
                    for i in range(2):
                        if not first:
                            pe.wait_ge(exp_done, 2 * s + i - 1)
                        if sub == 0:
                            nc.tensor.matmul(psS[:, i, :], identb[:], maskb[:].rearrange("p a b -> p (a b)"),
                                             start=True, stop=False, skip_group_check=True)
                        for b in (2 * i, 2 * i + 1):
                            c = slice(b * P, (b + 1) * P)
                            mm = product(psS[:, i, (b % 2) * D:(b % 2 + 1) * D], tuple(t[:, c] for t in q),
                                         tuple(flat(t[:, b, :, :]) for t in kd),
                                         sub == 1, True, skip_group_check=True)
                        mm.then_inc(s_mm, 1)

                def p_transposes(s):
                    for i in range(2):
                        pe.wait_ge(prob_done, 2 * s + i - 1)
                        for n in range(TPG):
                            mm = nc.tensor.transpose(psT[:, i, n * P:(n + 1) * P], prob[:, i * TPG + n, :], ident[:])
                        mm.then_inc(pT_mm, 1)

                def weighted_values(s, j):
                    c = slice(j * P, (j + 1) * P)
                    for i in range(2):
                        pe.wait_ge(pT_lo, 2 * s + i - 1)
                        for b in (2 * i, 2 * i + 1):
                            r = slice((b % 2) * D, (b % 2 + 1) * D)
                            mm = product(psT[:, i, r], tuple(t[:, b, c] for t in v), tuple(t[:, i, r] for t in pT),
                                         True, True, skip_group_check=True)
                    mm.then_inc(oT_mm, 1)

                def out_project(j, parity):
                    for t in range(TPG):
                        mm = product(psA[:, t // 2, (t % 2) * D:(t % 2 + 1) * D], tuple(o[:, parity, t, :] for o in oT),
                                     (wo_hi[:, j, :], wo_lo[:, j, :]), j == 0 and t % 2 == 0, j == PAIRS - 1,
                                     skip_group_check=True)
                    mm.then_inc(proj_mm, 1)

                def step(sub, G, j, after, depth=2):
                    s = G * PAIRS + j
                    scores(sub, s, first=depth == 0)
                    if depth > 0:
                        if depth > 1:
                            pe.wait_ge(oT_lo, 2 * s - 2)
                        p_transposes(s)
                    if j + 1 < PAIRS:
                        qk_project(sub, G, j + 1)
                    elif after < 2:
                        qk_project(after, G, j + 1)
                    if depth > 0:
                        if j == 1:
                            pe.wait_ge(v_lo, G * 2 * TPG + TPG)
                        if j == HP + 1:
                            pe.wait_ge(v_lo, G * 2 * TPG + 2 * TPG)
                        weighted_values(s, (j - 1) % PAIRS)
                    if depth > 1:
                        if j == 2:
                            pe.wait_ge(res_done, G + 1)
                            pe.wait_ge(w_lo, 8 if sub == 1 else 4)
                        if j == HP + 2 and sub == 1:
                            pe.wait_ge(w_lo, N_ATT)
                        out_project((j - 2) % PAIRS, j % 2)
                    if j < TPG:
                        pe.wait_ge(q_lo, s + 2)
                        v_project(sub, 1, j, 0)
                    if j == PAIRS - 2:
                        pe.wait_ge(q_lo, s + 2)
                        pe.wait_ge(k_lo, 2 * (s + 2))
                        z_transposes(pe, G + 1, psW)
                    if j == PAIRS - 1 and after < 2:
                        v_first_half(after, G + 1)

                z_transposes(pe, 0, psW)
                pe.wait_ge(w_lo, 1)
                qk_project(0, 0, 0)
                pe.wait_ge(w_lo, 3)
                v_first_half(0, 0)
                step(0, 0, 0, 0, depth=0)
                step(0, 0, 1, 0, depth=1)
                with pe.Fori(0, NGRP - 1) as G:
                    for j in range(2, PAIRS):
                        step(0, G, j, 0)
                    for j in range(2):
                        step(0, G + 1, j, 0)
                for j in range(2, PAIRS):
                    step(0, NGRP - 1, j, 1)
                for j in range(2):
                    step(1, NGRP, j, 1)
                with pe.Fori(NGRP, 2 * NGRP - 1) as G:
                    for j in range(2, PAIRS):
                        step(1, G, j, 1)
                    for j in range(2):
                        step(1, G + 1, j, 1)
                for j in range(2, PAIRS):
                    step(1, 2 * NGRP - 1, j, 2)
                pe.wait_ge(oT_lo, 2 * STEPS - 2)
                p_transposes(STEPS)
                out_project(PAIRS - 2, 0)
                weighted_values(STEPS, PAIRS - 1)
                pe.wait_ge(oT_lo, 2 * STEPS)
                out_project(PAIRS - 1, 1)

        ffn = ExitStack()
        with ffn:
            def fb(name, shape, dt=F32):
                return sb(name, shape, dt, ffn)

            wouts = [fb(f"wout_{n}", [P, HT, D], F32R) for n in ("hi", "lo")]
            wins = [fb(f"win_{n}", [P, KT, 2 * HID], F32R) for n in ("hi", "lo")]
            w2s = [fb(f"w2_{n}", [P, HT, NE * D], F32R) for n in ("hi", "lo")]
            earlier = fb("earlier", [P, NE, NE])
            hids = [fb(f"hid_{n}", [P, 2 * HT, GT], F32R) for n in ("hi", "lo")]
            silu = fb("silu", [P, 2, GT])
            h = fb("h", [P, 2, GT])
            logitsT = fb("logitsT", [NG, GT])
            logits = fb("logits", [P, TPG, NG])
            gmax = fb("gmax", [P, TPG])
            emax = fb("emax", [P, TPG, GROUPS])
            probs = fb("probs", [P, TPG, NG])
            gsum = fb("gsum", [P, TPG])
            esum = fb("esum", [P, TPG, GROUPS])
            chosen = fb("chosen", [P, TPG, GROUPS])
            coef = fb("coef", [P, TPG, GROUPS])
            above = fb("above", [P, TPG, NE, NE])
            ties = fb("ties", [P, TPG, NE, NE])
            rank = fb("rank", [P, TPG, NE])
            wse = fb("wse", [P, TPG, NE])
            acc = fb("acc", [P, 2, D])
            fin = fb("fin", [P, FIN, D])
            AB = [psS[:, 0, :], psS[:, 1, :], psW[:, 0, :], psW[:, 1, :]]
            OB = [psT[:, 0, :], psT[:, 1, :], psA[:, 0, :], psA[:, 1, :]]
            L0 = 2 * NGRP
            MT = 2 * HT
            GSTEPS = 19
            N0 = len(pieces)
            parts = [(wins[0][:], wins[1][:])] + \
                    [tuple(w[:, k, :].rearrange("p (e n) -> p e n", e=NE) for w in w2s) for k in range(HT)] + \
                    [(wouts[0][:], wouts[1][:])]
            late = [(src, *hl) for src, hl in zip(late_sources, parts)]
            LATE_AT = 0

            block2 = ffn.enter_context(nc.Block())

            @block2.sync
            def _(sp):
                for slot in stored:
                    sp.sem_inc(slot, 16)
                for i in range(STAGES, len(late)):
                    load(sp, N0 + i, late[i][0])
                with sp.Fori(0, NGRP) as g:
                    for t in range(TPG):
                        sp.wait_ge(fin_done, g * TPG + t + 1)
                        sp.dma_start(out[bass.ds((g * TPG + t) * P, P), :], fin[:, t % FIN, :]).then_inc(stored[t % FIN], 16)
                for slot in stored:
                    sp.wait_ge(slot, 16 * (B // FIN + 1))

            @block2.gpsimd
            def _(pool):
                nc.gpsimd.memset(earlier[:], 1.0).then_inc(ffn_ones, 1)
                pool.wait_ge(ffn_ones, 1)
                nc.gpsimd.affine_select(out=earlier[:], in_=earlier[:], compare_op=ALU.is_gt, fill=0.0, base=0,
                                        pattern=[[1, NE], [-1, NE]], channel_multiplier=0).then_inc(ffn_consts, 1)
                with pool.Fori(2 * NGRP + 1, 3 * NGRP) as g:
                    ln_scale(pool, g)

            @block2.scalar
            def _(act):
                def group(g, first=False):
                    if not first:
                        z_split_hi(act, g + L0, psS)
                    for m in range(MT):
                        act.wait_ge(ab_mm, g * MT + m + 1)
                        if not (first and m < 2):
                            act.wait_ge(h_done, g * MT + m - 1)
                        nc.scalar.activation(silu[:, m % 2, :], AB[2 * (m % 2)], ACT.Silu).then_inc(silu_done, 1)
                        if m >= 1:
                            split(g, m - 1)
                        if first and LATE_AT <= m < LATE_AT + len(late):
                            weights_hi(act, N0 + m - LATE_AT, late[m - LATE_AT][1])
                    split(g, MT - 1)
                    act.wait_ge(gate_step, g * GSTEPS + 4)
                    nc.scalar.activation(flat(probs[:]), flat(logits[:]), ACT.Exp).then_inc(gate_exp, 1)

                def split(g, m):
                    act.wait_ge(h_done, g * MT + m + 1)
                    nc.scalar.activation(hids[0][:, m, :], h[:, m % 2, :], ACT.Copy).then_inc(h_hi, 1)

                group(0, first=True)
                with act.Fori(1, NGRP) as g:
                    group(g)

            @block2.vector
            def _(dve):
                def gating(g):
                    count = [0]

                    def link(ins):
                        count[0] += 1
                        ins.then_inc(gate_step, 1)

                    def linked():
                        dve.wait_ge(gate_step, g * GSTEPS + count[0])

                    def wide(ap, n):
                        return ap.unsqueeze(len(ap.shape)).broadcast_to([*ap.shape, n])

                    lg = logits[:, :, 0:GROUPS]
                    le = logits[:, :, GROUPS:NG].rearrange("p t (g e) -> p t g e", g=GROUPS)
                    pg = probs[:, :, 0:GROUPS]
                    pe_ = probs[:, :, GROUPS:NG]
                    pe4 = pe_.rearrange("p t (g e) -> p t g e", g=GROUPS)
                    dve.wait_ge(gate_copied, g + 1)
                    link(nc.vector.tensor_reduce(gmax[:], lg, AX.X, ALU.max))
                    link(nc.vector.tensor_reduce(emax[:], le, AX.X, ALU.max))
                    linked()
                    link(nc.vector.tensor_tensor(lg, lg, wide(gmax[:], GROUPS), ALU.subtract))
                    link(nc.vector.tensor_tensor(le, le, wide(emax[:], PER_GROUP), ALU.subtract))
                    dve.wait_ge(gate_exp, g + 1)
                    link(nc.vector.tensor_reduce(gsum[:], pg, AX.X, ALU.add))
                    link(nc.vector.tensor_reduce(esum[:], pe4, AX.X, ALU.add))
                    linked()
                    link(nc.vector.reciprocal(gsum[:], gsum[:]))
                    link(nc.vector.reciprocal(esum[:], esum[:]))
                    linked()
                    link(nc.vector.tensor_tensor(pg, pg, wide(gsum[:], GROUPS), ALU.mult))
                    linked()
                    link(nc.vector.tensor_tensor(chosen[:, :, 0], pg[:, :, 0], pg[:, :, 1], ALU.is_ge))
                    link(nc.vector.tensor_tensor(chosen[:, :, 1], pg[:, :, 0], pg[:, :, 1], ALU.is_lt))
                    linked()
                    link(nc.vector.tensor_tensor(chosen[:], chosen[:], pg, ALU.mult))
                    linked()
                    link(nc.vector.tensor_tensor(coef[:], chosen[:], esum[:], ALU.mult))
                    linked()
                    link(nc.vector.tensor_tensor(pe4, pe4, wide(coef[:], PER_GROUP), ALU.mult))
                    linked()
                    this = wide(pe_, NE)
                    other = pe_.unsqueeze(2).broadcast_to([P, TPG, NE, NE])
                    link(nc.vector.tensor_tensor(above[:], other, this, ALU.is_gt))
                    link(nc.vector.tensor_tensor(ties[:], other, this, ALU.is_equal))
                    linked()
                    link(nc.vector.tensor_tensor(ties[:], ties[:],
                                                 earlier[:].unsqueeze(1).broadcast_to([P, TPG, NE, NE]), ALU.mult))
                    linked()
                    link(nc.vector.tensor_tensor(above[:], above[:], ties[:], ALU.add))
                    linked()
                    link(nc.vector.tensor_reduce(rank[:], above[:], AX.X, ALU.add))
                    linked()
                    assert count[0] == GSTEPS
                    nc.vector.scalar_tensor_tensor(wse[:], rank[:], TOP_K - 0.5, pe_, ALU.is_lt,
                                                   ALU.mult).then_inc(wse_done, 1)
                    dve.wait_ge(wse_done, g + 1)

                def hidden(g, first=False):
                    dve.wait_ge(gate_mm, g + 1)
                    nc.vector.tensor_scalar(logitsT[:], AB[2][0:NG, :], gbias[:, 0:1], None,
                                            ALU.add).then_inc(gate_biased, 1)
                    dve.wait_ge(gate_T, g + 1)
                    nc.vector.tensor_copy(flat(logits[:]), AB[3][:, 0:TPG * NG]).then_inc(gate_copied, 1)
                    for m in range(MT):
                        dve.wait_ge(silu_done, g * MT + m + 1)
                        if not (first and m < 2):
                            dve.wait_ge(h_lo, g * MT + m - 1)
                        nc.vector.tensor_tensor(h[:, m % 2, :], AB[2 * (m % 2) + 1], silu[:, m % 2, :],
                                                ALU.mult).then_inc(h_done, 1)
                        if m >= 1:
                            split(g, m - 1)
                        if first and LATE_AT <= m < LATE_AT + len(late):
                            i = m - LATE_AT
                            weights_lo(dve, N0 + i, late[i][2], late[i][1])
                    split(g, MT - 1)

                def split(g, m):
                    dve.wait_ge(h_hi, g * MT + m + 1)
                    nc.vector.tensor_tensor(hids[1][:, m, :], h[:, m % 2, :], hids[0][:, m, :].bitcast(F32),
                                            ALU.subtract).then_inc(h_lo, 1)

                def combine(g, t):
                    n0, a0 = g * TPG * OUTS + t * OUTS, (g * TPG + t + 1) * NE
                    chains = [fin[:, t % FIN, :], acc[:, t % 2, :]]
                    for c in range(OUTS - 1):
                        dve.wait_ge(out_mm, n0 + c + 1)
                        for i in range(2):
                            e = 2 * c + i
                            src, w, dst = OB[(t * OUTS + c) % 4][:, i * D:(i + 1) * D], wse[:, t, e:e + 1], chains[i]
                            if c:
                                dve.wait_ge(acc_done, a0 + e - 1)
                            if c == 0 and i == 0:
                                dve.wait_ge(stored[t % FIN], (g * (TPG // FIN) + t // FIN + 1) * 16)
                                ins = nc.vector.scalar_tensor_tensor(dst, src, w, row_tile(g, t), ALU.mult, ALU.add)
                            elif c == 0:
                                ins = nc.vector.tensor_scalar(dst, src, w, None, ALU.mult)
                            else:
                                ins = nc.vector.scalar_tensor_tensor(dst, src, w, dst, ALU.mult, ALU.add)
                            ins.then_inc(acc_done, 1)
                    dve.wait_ge(out_mm, n0 + OUTS)
                    dve.wait_ge(acc_done, a0 + NE)
                    nc.vector.tensor_tensor(chains[1], OB[(t * OUTS + OUTS - 1) % 4][:, 0:D], chains[1],
                                            ALU.add).then_inc(out_used, 1)
                    dve.wait_ge(out_used, g * TPG + t + 2)
                    nc.vector.tensor_tensor(chains[0], chains[0], chains[1], ALU.add).then_inc(fin_done, 1)

                def outputs(g, more=True):
                    combine(g, 0)
                    if more:
                        ln_stats(dve, g + 1 + L0, g + 1)
                    combine(g, 1)
                    if more:
                        ln_rows(dve, g + 1 + L0, g + 1)
                    combine(g, 2)
                    combine(g, 3)
                    if more:
                        z_split_lo(dve, g + 1 + L0, psS)

                dve.sem_inc(acc_done, NE)
                dve.sem_inc(out_used, 1)
                dve.wait_ge(ffn_consts, 1)
                dve.wait_ge(res_done, L0 + 1)
                hidden(0, first=True)
                gating(0)
                with dve.Fori(0, NGRP - 1) as g:
                    outputs(g)
                    hidden(g + 1)
                    gating(g + 1)
                outputs(NGRP - 1, more=False)

            @block2.tensor
            def _(pe):
                def hidden(g):
                    pe.wait_ge(z_lo, (g + L0 + 1) * KT)
                    for k in range(KT):
                        mm = product(AB[2][0:NG, :], (gws[0][:, k, :], gws[1][:, k, :]), (zhi[:, k, :], zlo[:, k, :]),
                                     k == 0, k == KT - 1)
                    mm.then_inc(gate_mm, 1)
                    for m in range(MT):
                        ws = w1s if m < HT else wins
                        if m == HT:
                            pe.wait_ge(w_lo, N0 + 1)
                        if m == 1:
                            pe.wait_ge(gate_copied, g + 1)
                        if m >= 2:
                            pe.wait_ge(h_done, g * MT + m - 1)
                        for half in range(2):
                            c = slice(half * HID + (m % HT) * P, half * HID + (m % HT + 1) * P)
                            for k in range(KT):
                                if m == 0 and (half, k) == (1, KT - 1):
                                    pe.wait_ge(gate_biased, g + 1)
                                mm = product(AB[2 * (m % 2) + half], (ws[0][:, k, c], ws[1][:, k, c]),
                                             (zhi[:, k, :], zlo[:, k, :]), k == 0, k == KT - 1)
                        mm.then_inc(ab_mm, 1)
                        if m == 0:
                            for t in range(TPG):
                                mm = nc.tensor.transpose(AB[3][:, t * NG:(t + 1) * NG], logitsT[:, t * P:(t + 1) * P],
                                                         ident[0:NG, 0:NG])
                            mm.then_inc(gate_T, 1)

                def outputs(g, more=True):
                    for t in range(TPG):
                        r = slice(t * P, (t + 1) * P)
                        for c in range(OUTS):
                            n = t * OUTS + c
                            shared = c == OUTS - 1
                            if t == 0:
                                if c == 0:
                                    pe.wait_ge(w_lo, N0 + 1 + HT)
                                    pe.wait_ge(h_lo, g * MT + HT)
                                if shared:
                                    pe.wait_ge(w_lo, N0 + len(late))
                                    pe.wait_ge(h_lo, g * MT + MT)
                            back, place = (n - 4) // OUTS, (n - 4) % OUTS
                            if place == OUTS - 1:
                                pe.wait_ge(out_used, g * TPG + back + 2)
                            else:
                                pe.wait_ge(acc_done, (g * TPG + back + 1) * NE + 2 * place + 2)
                            for k in range(HT):
                                m = HT + k if shared else k
                                lhs = (hids[0][:, m, r], hids[1][:, m, r])
                                cols_ = slice(c * 2 * D, (c + 1) * 2 * D)
                                rhs = tuple(w[:, k, :] for w in wouts) if shared else tuple(w[:, k, cols_] for w in w2s)
                                dst = OB[n % 4][:, 0:D] if shared else OB[n % 4]
                                mm = product(dst, lhs, rhs, k == 0, k == HT - 1)
                            mm.then_inc(out_mm, 1)
                        if t == 2 and more:
                            pe.wait_ge(h_done, (g + 1) * MT)
                            z_transposes(pe, g + 1 + L0, psS)

                pe.wait_ge(gate_in, 32)
                pe.wait_ge(g_lo, 1)
                pe.wait_ge(w_lo, N0)
                pe.wait_ge(res_done, L0 + 1)
                hidden(0)
                with pe.Fori(0, NGRP - 1) as g:
                    outputs(g)
                    hidden(g + 1)
                outputs(NGRP - 1, more=False)


def kernel(**inputs):
    import numpy as _np
    import concourse.bacc as _bacc
    from concourse import mybir as _mybir
    from concourse.bass_utils import run_bass_kernel_spmd as _run

    def c(a):
        return _np.ascontiguousarray(a)

    a = {k: _np.asarray(v) for k, v in inputs.items()}
    tokens = a["x"].shape[0] * a["x"].shape[1]
    d = a["x"].shape[2]
    w2 = a["L0_ffn_w2"]
    arrays = {
        "x": c(a["x"].reshape(tokens, d)),
        "ctxT": c(a["ctx_1024"].reshape(tokens, d).T),
        "wq": c(a["L0_attn_Wq"]), "wk": c(a["L0_attn_Wk"]), "wv": c(a["L0_attn_Wv"]), "wr": c(a["L0_attn_Wr"]),
        "xq": c(a["L0_xattn_w_q"]), "xk": c(a["L0_xattn_w_k"]), "xv": c(a["L0_xattn_w_v"]), "xr": c(a["L0_xattn_w_o"]),
        "w1": c(a["L0_ffn_w1"].T), "win": c(a["L0_ffn_w_in"].T), "wout": c(a["L0_ffn_w_out"].T),
        "w2": c(w2.transpose(2, 0, 1).reshape(w2.shape[2], w2.shape[0] * w2.shape[1])),
        "wgate": c(_np.concatenate([a["L0_ffn_wg"], a["L0_ffn_we"]], 0).T),
        "bgate": c(_np.concatenate([a["L0_ffn_gb"], a["L0_ffn_eb"]])[:, None]),
    }
    nc = _bacc.Bacc("TRN2", target_bir_lowering=False, num_devices=1)
    args = [nc.dram_tensor(n, v.shape, _mybir.dt.from_np(v.dtype), kind="ExternalInput").ap() for n, v in arrays.items()]
    out = nc.dram_tensor("out", (tokens, d), _mybir.dt.float32, kind="ExternalOutput").ap()
    build(nc, *args, out)
    r = _run(nc, [arrays], core_ids=[0])
    return r.results[0]["out"].reshape(a["x"].shape)
```

```python
from contextlib import ExitStack

import concourse.bass as bass
from concourse import mybir

F32 = mybir.dt.float32
F32R = mybir.dt.float32r
ACT = mybir.ActivationFunctionType
ALU = mybir.AluOpType
AX = mybir.AxisListType

P = 128
B, S, D = 16, 128, 256
HEADS, HD = 16, 64
INNER = HEADS * HD
HID = 512
GROUPS, PER_GROUP = 2, 4
NE = GROUPS * PER_GROUP
NG = GROUPS + NE
TOP_K = 2
EPS = 1e-5
MASK = -50.0
SCALE = HD ** -0.5
LARGE = 3e38

TPG = 4
GT = TPG * P
NGRP = B // TPG
KT = D // P
PAIRS = HEADS // 2
HT = HID // P
CHUNK = KT * INNER
WARM = 13
STAGES = 3
FIN = 2
OUTS = NE // 2 + 1


def build(nc, x, ctxT, wq, wk, wv, wr, xq, xk, xv, xr, w1, win, wout, w2, wgate, bgate, out):
    ctx = ExitStack()
    with ctx:
        def sem(name):
            return ctx.enter_context(nc.semaphore(name))

        def sb(name, shape, dt=F32, stack=ctx):
            return stack.enter_context(nc.sbuf_tensor(name, shape, dt))

        def ps(name):
            return ctx.enter_context(nc.psum_tensor(name, [P, 2, 512], F32))

        xres = sb("xres", [P, B, D])
        stage = sb("stage", [P, STAGES, CHUNK])
        ident = sb("ident", [P, P])
        mask = sb("mask", [P, P])
        z = sb("z", [P, TPG, D])
        zhi = sb("zhi", [P, KT, GT], F32R)
        zlo = sb("zlo", [P, KT, GT], F32R)
        bnst = sb("bnst", [P, TPG, 6])
        mv = sb("mv", [P, TPG, 2])
        veps = sb("veps", [P, TPG])
        rstd = sb("rstd", [P, TPG])
        mhalf = sb("mhalf", [P, TPG])
        eps = sb("eps", [P, TPG])
        psS, psW, psT, psA = ps("psS"), ps("psW"), ps("psT"), ps("psA")

        x_first = [sem(f"x_first{t}") for t in range(TPG)]
        x_in = [sem(f"x_in{g}") for g in range(1, NGRP)]
        stage_in = [sem(f"stage_in{k}") for k in range(STAGES)]
        gate_in, ctx_in = sem("gate_in"), sem("ctx_in")
        zeroed, consts, ffn_ones, ffn_consts = sem("zeroed"), sem("consts"), sem("ffn_ones"), sem("ffn_consts")
        w_hi, w_lo, w_lo_pool = sem("w_hi"), sem("w_lo"), sem("w_lo_pool")
        g_hi, g_lo = sem("g_hi"), sem("g_lo")
        c_hi, c_lo = sem("c_hi"), sem("c_lo")
        bn_done, bn_seen, mv_done, eps_done, rstd_done, z_done = (
            sem("bn_done"), sem("bn_seen"), sem("mv_done"), sem("eps_done"), sem("rstd_done"), sem("z_done"))
        rstd_seen, z_centred = sem("rstd_seen"), sem("z_centred")
        zT_mm, z_hi, z_lo = sem("zT_mm"), sem("z_hi"), sem("z_lo")
        qk_mm, q_hi, q_lo, k_hi, k_lo = sem("qk_mm"), sem("q_hi"), sem("q_lo"), sem("k_hi"), sem("k_lo")
        v_mm, v_hi, v_lo = sem("v_mm"), sem("v_hi"), sem("v_lo")
        s_seen = sem("s_seen")
        s_mm, min_done, exp_done, recip_done, prob_done = (
            sem("s_mm"), sem("min_done"), sem("exp_done"), sem("recip_done"), sem("prob_done"))
        pT_mm, pT_hi, pT_lo = sem("pT_mm"), sem("pT_hi"), sem("pT_lo")
        oT_mm, oT_hi, oT_lo = sem("oT_mm"), sem("oT_hi"), sem("oT_lo")
        proj_mm, res_done = sem("proj_mm"), sem("res_done")
        gate_mm, gate_biased, gate_T, gate_copied, gate_step, gate_exp, wse_done = (
            sem("gate_mm"), sem("gate_biased"), sem("gate_T"), sem("gate_copied"), sem("gate_step"), sem("gate_exp"), sem("wse_done"))
        ab_mm, silu_done, h_done, h_hi, h_lo = (
            sem("ab_mm"), sem("silu_done"), sem("h_done"), sem("h_hi"), sem("h_lo"))
        out_mm, out_used, acc_done, fin_done = sem("out_mm"), sem("out_used"), sem("acc_done"), sem("fin_done")
        stored = [sem(f"stored{i}") for i in range(FIN)]

        def flat(ap):
            return ap.rearrange("p a b -> p (a b)")

        def rows(g):
            return xres[:, bass.ds(g * TPG, TPG), :]

        def row_tile(g, t):
            return flat(xres[:, bass.ds(g * TPG + t, 1), :])

        def product(o, lhs, rhs, start, stop, **kw):
            (lh, ll), (rh, rl) = lhs, rhs
            nc.tensor.matmul(o, lh, rl, start=start, stop=False, **kw)
            nc.tensor.matmul(o, lh, rh, start=False, stop=False, **kw)
            return nc.tensor.matmul(o, ll, rh, start=False, stop=stop, **kw)

        def ln_stats(dve, g, row_g, loaded=()):
            for t in range(TPG):
                if loaded:
                    dve.wait_ge(loaded[t], 16)
                nc.vector.bn_stats(bnst[:, t, :], row_tile(row_g, t)).then_inc(bn_done, 1)
            dve.wait_ge(bn_done, (g + 1) * TPG)
            dve.sem_inc(bn_seen, 1)
            for t in range(TPG):
                nc.vector.bn_aggr(mv[:, t, :], bnst[:, t, :]).then_inc(mv_done, 1)

        def ln_rows(dve, g, row_g):
            dve.wait_ge(rstd_done, g + 1)
            if not (isinstance(g, int) and g == 0):
                dve.wait_ge(zT_mm, g * KT)
            for t in range(TPG):
                nc.vector.tensor_scalar(z[:, t, :], row_tile(row_g, t), mv[:, t, 0:1], rstd[:, t:t + 1],
                                        ALU.subtract, ALU.mult).then_inc(z_done, 1)

        def ln_scale(pool, g):
            pool.wait_ge(mv_done, (g + 1) * TPG)
            nc.gpsimd.tensor_tensor(veps[:], mv[:, :, 1], eps[:], ALU.add).then_inc(eps_done, 1)
            pool.wait_ge(eps_done, g + 1)
            nc.gpsimd.tensor_tensor(rstd[:], veps[:], mhalf[:], ALU.pow).then_inc(rstd_done, 1)

        def ln_rows_pool(pool, g, row_g, tiles):
            if 0 in tiles:
                pool.wait_ge(rstd_done, g + 1)
                pool.wait_ge(zT_mm, g * KT)
                pool.sem_inc(rstd_seen, 1)
            for t in tiles:
                nc.gpsimd.tensor_tensor(z[:, t, :], row_tile(row_g, t), mv[:, t, 0:1].broadcast_to([P, D]),
                                        ALU.subtract).then_inc(z_centred, 1)
            pool.wait_ge(z_centred, g * TPG + tiles[-1] + 1 - TPG)
            for t in tiles:
                nc.gpsimd.tensor_tensor(z[:, t, :], z[:, t, :], rstd[:, t:t + 1].broadcast_to([P, D]),
                                        ALU.mult).then_inc(z_done, 1)

        def z_transposes(pe, g, banks):
            pe.wait_ge(z_done, (g + 1) * TPG)
            for k in range(KT):
                for t in range(TPG):
                    mm = nc.tensor.transpose(banks[:, k, t * P:(t + 1) * P], z[:, t, k * P:(k + 1) * P], ident[:])
                mm.then_inc(zT_mm, 1)

        def z_split_hi(act, g, banks):
            for k in range(KT):
                act.wait_ge(zT_mm, g * KT + k + 1)
                nc.scalar.activation(zhi[:, k, :], banks[:, k, :], ACT.Copy).then_inc(z_hi, 1)

        def z_split_lo(dve, g, banks):
            for k in range(KT):
                dve.wait_ge(z_hi, g * KT + k + 1)
                nc.vector.tensor_tensor(zlo[:, k, :], banks[:, k, :], zhi[:, k, :].bitcast(F32),
                                        ALU.subtract).then_inc(z_lo, 1)

        def residual(dve, G, sub):
            dve.wait_ge(proj_mm, (G + 1) * PAIRS)
            for i in range(2):
                half = flat(xres[:, bass.ds((G - sub * NGRP) * TPG + 2 * i, 2), :])
                r = nc.vector.tensor_tensor(half, psA[:, i, :], half, ALU.add)
            r.then_inc(res_done, 1)

        L0 = 2 * NGRP
        MT = 2 * HT
        AB = [psS[:, 0, :], psS[:, 1, :], psW[:, 0, :], psW[:, 1, :]]

        def gate_logits(pe, g):
            pe.wait_ge(z_lo, (g + L0 + 1) * KT)
            for k in range(KT):
                mm = product(AB[2][0:NG, :], (gws[0][:, k, :], gws[1][:, k, :]), (zhi[:, k, :], zlo[:, k, :]),
                             k == 0, k == KT - 1)
            mm.then_inc(gate_mm, 1)

        def hidden_half(ws, m, half, k):
            c = slice(half * HID + (m % HT) * P, half * HID + (m % HT + 1) * P)
            return product(AB[2 * (m % 2) + half], (ws[0][:, k, c], ws[1][:, k, c]),
                           (zhi[:, k, :], zlo[:, k, :]), k == 0, k == KT - 1)

        w1s = [sb(f"w1_{n}", [P, KT, 2 * HID], F32R) for n in ("hi", "lo")]
        graw = sb("graw", [P, KT, NG])
        gbias = sb("gbias", [NG, 1])
        gws = [sb(f"gw_{n}", [P, KT, NG], F32R) for n in ("hi", "lo")]

        PIECES = [f"{w} {half}" for w, half in
                  (("wq", "lower"), ("wk", "lower"), ("wv", "lower"), ("wv", "upper"), ("wq", "upper"), ("wr", "lower"),
                   ("wk", "upper"), ("wr", "upper"),
                   ("xq", "lower"), ("xk", "lower"), ("xv", "lower"), ("xv", "upper"), ("xr", "lower"), ("xq", "upper"),
                   ("xk", "upper"), ("xr", "upper"), ("w1", "lower"), ("w1", "upper"))]
        PIECES += ["win"] + [f"w2 {k}" for k in range(HT)] + ["wout"]
        BY_POOL = ("wk upper", "wr lower", "wr upper", "xv upper", "xr lower", "xk upper", "xr upper",
                   "w1 lower", "win", "w2 0", "w2 2")

        def wait_lo(eng, name):
            before = PIECES[:PIECES.index(name) + 1]
            by_pool = sum(n in BY_POOL for n in before)
            if name in BY_POOL:
                eng.wait_ge(w_lo_pool, by_pool)
            else:
                eng.wait_ge(w_lo, len(before) - by_pool)

        def piece(n, shape):
            return stage[:, n % STAGES, 0:shape[1] * shape[2]].rearrange("p (a b) -> p a b", a=shape[1])

        def load(sp, n, src):
            if n >= STAGES:
                wait_lo(sp, PIECES[n - STAGES])
            sp.dma_start(piece(n, src.shape), src).then_inc(stage_in[n % STAGES], 16)

        def weights_hi(act, n, dst, scale=1.0):
            act.wait_ge(stage_in[n % STAGES], 16 * (n // STAGES + 1))
            nc.scalar.activation(dst, piece(n, dst.shape), ACT.Copy, scale=scale).then_inc(w_hi, 1)

        def weights_lo(dve, n, dst, hi, scale=1.0):
            dve.wait_ge(w_hi, n + 1)
            nc.vector.scalar_tensor_tensor(dst, piece(n, dst.shape), scale, hi.bitcast(F32),
                                           ALU.mult, ALU.subtract).then_inc(w_lo, 1)

        def weights_lo_pool(pool, n, dst, hi):
            pool.wait_ge(w_hi, n + 1)
            nc.gpsimd.tensor_tensor(dst, piece(n, dst.shape), hi.bitcast(F32), ALU.subtract).then_inc(w_lo_pool, 1)

        def k_rows(w):
            return w.rearrange("(k p) n -> p k n", p=P)

        w2_rows = w2.rearrange("(k p) (e n) -> k p e n", p=P, e=NE)

        att = ExitStack()
        with att:
            def ab(name, shape, dt=F32):
                return sb(name, shape, dt, att)

            wh = [ab(f"w{n}_hi", [P, KT, INNER], F32R) for n in "qkv"]
            wl = [ab(f"w{n}_lo", [P, KT, INNER], F32R) for n in "qkv"]
            wo_hi = ab("wo_hi", [P, PAIRS, D], F32R)
            wo_lo = ab("wo_lo", [P, PAIRS, D], F32R)
            craw = stage[:, 2, CHUNK // 2:].rearrange("p (k t) -> p k t", k=KT)
            chi = ab("chi", [P, KT, GT], F32R)
            clo = ab("clo", [P, KT, GT], F32R)
            q = [ab(f"q_{n}", [P, GT], F32R) for n in ("hi", "lo")]
            kd = [ab(f"kd_{n}", [P, TPG, 2, P], F32R) for n in ("hi", "lo")]
            v = [ab(f"v_{n}", [P, TPG, INNER], F32R) for n in ("hi", "lo")]
            nmin = ab("nmin", [P, TPG * 2])
            prob = ab("prob", [P, TPG * 2, P])
            psums = ab("psums", [P, TPG * 2])
            rsum = ab("rsum", [P, TPG * 2])
            pT = [ab(f"pT_{n}", [P, 2, GT], F32R) for n in ("hi", "lo")]
            oT = [ab(f"oT_{n}", [P, 2, TPG, P], F32R) for n in ("hi", "lo")]
            Q, K, V = 0, 1, 2
            HC, HP = INNER // 2, PAIRS // 2
            lower, upper = slice(0, HC), slice(HC, INNER)

            def columns(w, src, c, scale):
                return (k_rows(src)[:, :, c], wh[w][:, :, c], wl[w][:, :, c], scale)

            def pair_rows(src, r):
                return (k_rows(src)[:, r, :], wo_hi[:, r, :], wo_lo[:, r, :], 1.0)

            pieces = [columns(Q, wq, lower, -SCALE), columns(K, wk, lower, 1.0), columns(V, wv, lower, 1.0),
                       columns(V, wv, upper, 1.0), columns(Q, wq, upper, -SCALE), pair_rows(wr, slice(0, HP)),
                       columns(K, wk, upper, 1.0), pair_rows(wr, slice(HP, PAIRS))]
            N_SELF = len(pieces)
            pieces += [columns(Q, xq, lower, -SCALE), columns(K, xk, lower, 1.0),
                       columns(V, xv, lower, 1.0), columns(V, xv, upper, 1.0), pair_rows(xr, slice(0, HP)),
                       columns(Q, xq, upper, -SCALE), columns(K, xk, upper, 1.0), pair_rows(xr, slice(HP, PAIRS))]
            N_ATT = len(pieces)
            pieces += [(k_rows(w1)[:, :, c], w1s[0][:, :, c], w1s[1][:, :, c], 1.0) for c in (lower, upper)]
            late_sources = [k_rows(win)] + [w2_rows[k] for k in range(HT)] + [k_rows(wout)]
            SWAPS = {(0, 0): ("wq upper", "wr lower"), (0, 1): ("wk upper",), (0, 2): ("wr upper",),
                     (NGRP - 1, 3): ("xq lower",), (NGRP - 1, 4): ("xk lower",), (NGRP - 1, 5): ("xv lower",),
                     (NGRP - 1, 7): ("xv upper",), (NGRP, 0): ("xr lower", "xq upper"), (NGRP, 1): ("xk upper",),
                     (NGRP, 2): ("xr upper",), (2 * NGRP - 1, 3): ("w1 lower",), (2 * NGRP - 1, 5): ("w1 upper",)}
            assert len(pieces) == PIECES.index("win")
            STEPS = 2 * NGRP * PAIRS
            PEEL = 3
            LN_AT = PEEL
            GATE_AT = (2 * NGRP - 1, 4)
            N_CONST = 6
            head_rows = [slice(h * HD, (h + 1) * HD) for h in range(2)]

            def banks(pair):
                return flat(pair[:]).rearrange("p (b h q) -> p b h q", b=TPG, h=2)

            def swaps(G, j):
                return [(PIECES.index(n), n in BY_POOL) for n in SWAPS.get((G, j), ())] if isinstance(G, int) else []

            block = att.enter_context(nc.Block())

            @block.sync
            def _(sp):
                xv_ = x.rearrange("(g t p) d -> g p t d", p=P, t=TPG)
                for t in range(TPG):
                    sp.dma_start(xres[:, t, :], xv_[0][:, t, :]).then_inc(x_first[t], 16)

                for n in range(STAGES):
                    load(sp, n, pieces[n][0])
                ctx_v = ctxT.rearrange("(k p) t -> p k t", p=P)
                sp.dma_start(graw[:], k_rows(wgate)).then_inc(gate_in, 16)
                sp.dma_start(gbias[:], bgate).then_inc(gate_in, 16)
                for n in range(STAGES, 2 * STAGES):
                    load(sp, n, pieces[n][0])
                for g in range(1, NGRP):
                    sp.dma_start(xres[:, g * TPG:(g + 1) * TPG, :], xv_[g]).then_inc(x_in[g - 1], 16)
                for n in range(2 * STAGES, N_SELF):
                    load(sp, n, pieces[n][0])
                sp.dma_start(craw, ctx_v[:, :, 0:GT]).then_inc(ctx_in, 16)
                for n in range(N_SELF, N_ATT):
                    load(sp, n, pieces[n][0])
                for g in range(1, NGRP):
                    sp.wait_ge(c_lo, g)
                    sp.dma_start(craw, ctx_v[:, :, g * GT:(g + 1) * GT]).then_inc(ctx_in, 16)
                sp.wait_ge(c_lo, NGRP)
                for n in range(N_ATT, len(pieces)):
                    load(sp, n, pieces[n][0])
                for i in range(STAGES):
                    load(sp, len(pieces) + i, late_sources[i])

            @block.gpsimd
            def _(pool):
                nc.gpsimd.memset(ident[:], 0.0).then_inc(zeroed, 1)
                nc.gpsimd.memset(mask[:], 0.0).then_inc(zeroed, 1)
                nc.gpsimd.memset(mhalf[:], -0.5).then_inc(consts, 1)
                nc.gpsimd.memset(eps[:], EPS).then_inc(consts, 1)
                for t in kd:
                    nc.gpsimd.memset(t[:].bitcast(F32), 0.0).then_inc(consts, 1)
                pool.wait_ge(zeroed, 2)
                nc.gpsimd.affine_select(out=ident[:], in_=ident[:], compare_op=ALU.not_equal, fill=1.0, base=0,
                                        pattern=[[-1, P]], channel_multiplier=1).then_inc(consts, 1)
                nc.gpsimd.affine_select(out=mask[:], in_=mask[:], compare_op=ALU.is_ge, fill=-MASK, base=0,
                                        pattern=[[-1, P]], channel_multiplier=1).then_inc(consts, 1)
                pool.wait_ge(consts, N_CONST)

                def step(G, j, after):
                    s = G * PAIRS + j
                    for i in range(2):
                        pool.wait_ge(recip_done, 2 * s + i + 1)
                        r = slice(i * TPG, (i + 1) * TPG)
                        nc.gpsimd.tensor_tensor(prob[:, r, :], prob[:, r, :],
                                                rsum[:, r].unsqueeze(2).broadcast_to([P, TPG, P]),
                                                ALU.mult).then_inc(prob_done, 1)
                    if j == PAIRS - 2 and after == 1:
                        pool.wait_ge(c_hi, G + 2 - NGRP)
                        nc.gpsimd.tensor_tensor(flat(clo[:]), flat(craw), flat(chi[:]).bitcast(F32),
                                                ALU.subtract).then_inc(c_lo, 1)
                    if j == LN_AT:
                        ln_scale(pool, G + 1)
                    if j in (LN_AT + 1, LN_AT + 2):
                        t = (j - LN_AT - 1) * 2
                        ln_rows_pool(pool, G + 1, G + 1 - after * NGRP, range(t, t + 2))
                    for n, by_pool in swaps(G, j):
                        _, hi, lo, _ = pieces[n]
                        if by_pool:
                            weights_lo_pool(pool, n, lo, hi)

                ln_scale(pool, 0)
                for j in range(PEEL):
                    step(0, j, 0)
                with pool.Fori(0, NGRP - 1) as G:
                    for j in range(PEEL, PAIRS):
                        step(G, j, 0)
                    for j in range(PEEL):
                        step(G + 1, j, 0)
                for j in range(PEEL, PAIRS):
                    step(NGRP - 1, j, 1)
                for j in range(PEEL):
                    step(NGRP, j, 1)
                with pool.Fori(NGRP, 2 * NGRP - 1) as G:
                    for j in range(PEEL, PAIRS):
                        step(G, j, 1)
                    for j in range(PEEL):
                        step(G + 1, j, 1)
                for j in range(PEEL, PAIRS):
                    step(2 * NGRP - 1, j, 2)

            @block.scalar
            def _(act):
                act.preload_act_table(ACT.Exp)

                def split_context(cg):
                    act.wait_ge(ctx_in, (cg + 1) * 16)
                    nc.scalar.activation(flat(chi[:]), flat(craw), ACT.Copy).then_inc(c_hi, 1)

                def qk_split(G, j):
                    n = G * PAIRS + j
                    act.wait_ge(qk_mm, 2 * n + 1)
                    nc.scalar.activation(q[0][:], psW[:, Q, :], ACT.Copy).then_inc(q_hi, 1)
                    act.wait_ge(qk_mm, 2 * n + 2)
                    for h, r in enumerate(head_rows):
                        nc.scalar.activation(kd[0][r, :, h, :], psW[r, K, :].rearrange("p (b k) -> p b k", b=TPG),
                                             ACT.Copy).then_inc(k_hi, 1)

                def v_split(G, half, t, bank):
                    act.wait_ge(v_mm, G * 2 * TPG + half * TPG + t + 1)
                    nc.scalar.activation(v[0][:, t, half * HC:(half + 1) * HC], psW[:, bank, :], ACT.Copy).then_inc(v_hi, 1)

                def pT_split(s):
                    for i in range(2):
                        act.wait_ge(pT_mm, 2 * s + i - 1)
                        nc.scalar.activation(pT[0][:, i, :], psT[:, i, :], ACT.Copy).then_inc(pT_hi, 1)

                def oT_split(s, parity, i):
                    act.wait_ge(oT_mm, 2 * s + i - 1)
                    b = slice(2 * i, 2 * i + 2)
                    for h, r in enumerate(head_rows):
                        nc.scalar.activation(oT[0][r, parity, b, :], banks(psT)[r, b, h, :], ACT.Copy).then_inc(oT_hi, 1)

                def step(G, j, after, first=False):
                    s = G * PAIRS + j
                    if not first:
                        pT_split(s)
                    for i in range(2):
                        act.wait_ge(min_done, 2 * s + i + 1)
                        if not first:
                            act.wait_ge(pT_mm, 2 * s + i - 1)
                        for n in range(i * TPG, (i + 1) * TPG):
                            e = nc.scalar.activation(prob[:, n, :], flat(psS[:])[:, n * P:(n + 1) * P], ACT.Exp,
                                                     bias=nmin[:, n:n + 1], scale=-1.0, accum_out=psums[:, n:n + 1])
                        e.then_inc(exp_done, 1)
                        if i == 0 and (j + 1 < PAIRS or after < 2):
                            qk_split(G, j + 1)
                            if j == PAIRS - 2 and after == 1:
                                split_context(G + 1 - NGRP)
                        if not first:
                            oT_split(s, (j + 1) % 2, i)
                    if j < TPG:
                        v_split(G, 1, j, 0)
                    if j == PAIRS - 2:
                        z_split_hi(act, G + 1, psW)
                    if j == PAIRS - 1 and after < 2:
                        for t in range(TPG):
                            v_split(G + 1, 0, t, t % 2)
                    for n, _ in swaps(G, j):
                        if n == N_ATT - 1:
                            act.wait_ge(proj_mm, NGRP * PAIRS)
                        _, hi, _, scale = pieces[n]
                        weights_hi(act, n, hi, scale)
                    if isinstance(G, int) and (G, j) == GATE_AT:
                        act.wait_ge(gate_in, 32)
                        nc.scalar.activation(gws[0][:], graw[:], ACT.Copy).then_inc(g_hi, 1)

                def first_hi(n):
                    weights_hi(act, n, pieces[n][1], pieces[n][3])

                first_hi(Q)
                z_split_hi(act, 0, psW)
                first_hi(K)
                first_hi(V)
                qk_split(0, 0)
                for t in range(TPG):
                    v_split(0, 0, t, t % 2)
                    if t == 0:
                        first_hi(3)
                step(0, 0, 0, first=True)
                for j in range(1, PEEL):
                    step(0, j, 0)
                with act.Fori(0, NGRP - 1) as G:
                    for j in range(PEEL, PAIRS):
                        step(G, j, 0)
                    for j in range(PEEL):
                        step(G + 1, j, 0)
                for j in range(PEEL, PAIRS):
                    step(NGRP - 1, j, 1)
                for j in range(PEEL):
                    step(NGRP, j, 1)
                with act.Fori(NGRP, 2 * NGRP - 1) as G:
                    for j in range(PEEL, PAIRS):
                        step(G, j, 1)
                    for j in range(PEEL):
                        step(G + 1, j, 1)
                for j in range(PEEL, PAIRS):
                    step(2 * NGRP - 1, j, 2)
                pT_split(STEPS)
                for i in range(2):
                    oT_split(STEPS, 1, i)

            @block.vector
            def _(dve):
                def qk_split(G, j):
                    n = G * PAIRS + j
                    dve.wait_ge(q_hi, n + 1)
                    nc.vector.tensor_tensor(q[1][:], psW[:, Q, :], q[0][:].bitcast(F32), ALU.subtract).then_inc(q_lo, 1)
                    for h, r in enumerate(head_rows):
                        dve.wait_ge(k_hi, 2 * n + h + 1)
                        nc.vector.tensor_tensor(kd[1][r, :, h, :], psW[r, K, :].rearrange("p (b k) -> p b k", b=TPG),
                                                kd[0][r, :, h, :].bitcast(F32), ALU.subtract).then_inc(k_lo, 1)

                def v_split(G, half, t, bank):
                    dve.wait_ge(v_hi, G * 2 * TPG + half * TPG + t + 1)
                    c = slice(half * HC, (half + 1) * HC)
                    nc.vector.tensor_tensor(v[1][:, t, c], psW[:, bank, :], v[0][:, t, c].bitcast(F32),
                                            ALU.subtract).then_inc(v_lo, 1)

                def pT_split(s):
                    for i in range(2):
                        dve.wait_ge(pT_hi, 2 * s + i - 1)
                        nc.vector.tensor_tensor(pT[1][:, i, :], psT[:, i, :], pT[0][:, i, :].bitcast(F32),
                                                ALU.subtract).then_inc(pT_lo, 1)

                def oT_split(s, parity, i):
                    b = slice(2 * i, 2 * i + 2)
                    for h, r in enumerate(head_rows):
                        dve.wait_ge(oT_hi, 4 * s - 3 + 2 * i + h)
                        nc.vector.tensor_tensor(oT[1][r, parity, b, :], banks(psT)[r, b, h, :],
                                                oT[0][r, parity, b, :].bitcast(F32), ALU.subtract).then_inc(oT_lo, 1)

                def step(G, j, after, causal=True, first=False, sub=0):
                    s = G * PAIRS + j
                    row_g = G + 1 - after * NGRP
                    for i in range(2):
                        dve.wait_ge(s_mm, 2 * s + i + 1)
                        r = slice(i * TPG, (i + 1) * TPG)
                        if causal:
                            dve.sem_inc(s_seen, 1)
                            for n in range(TPG):
                                sc = psS[:, i, n * P:(n + 1) * P]
                                m = nc.vector.tensor_tensor_reduce(sc, sc, mask[:], 1.0, LARGE, ALU.add, ALU.min,
                                                                   nmin[:, i * TPG + n:i * TPG + n + 1])
                        else:
                            m = nc.vector.tensor_reduce(nmin[:, r], psS[:, i, :].rearrange("p (n k) -> p n k", k=P),
                                                        AX.X, ALU.min)
                        m.then_inc(min_done, 1)
                    if not first:
                        pT_split(s)
                    if j == LN_AT:
                        if after:
                            dve.wait_ge(res_done, (G + 2 - NGRP if isinstance(G, int) else NGRP) + 1)
                        ln_stats(dve, G + 1, row_g)
                    for i in range(2):
                        dve.wait_ge(exp_done, 2 * s + i + 1)
                        r = slice(i * TPG, (i + 1) * TPG)
                        nc.vector.reciprocal(rsum[:, r], psums[:, r]).then_inc(recip_done, 1)
                        if i == 0 and (j + 1 < PAIRS or after < 2):
                            qk_split(G, j + 1)
                        if not first:
                            oT_split(s, (j + 1) % 2, i)
                    if j == 1 and not (isinstance(G, int) and G == 0):
                        residual(dve, G - 1, sub)
                    if j < TPG:
                        v_split(G, 1, j, 0)
                    if j == PAIRS - 2:
                        z_split_lo(dve, G + 1, psW)
                    if j == PAIRS - 1 and after < 2:
                        for t in range(TPG):
                            v_split(G + 1, 0, t, t % 2)
                    for n, by_pool in swaps(G, j):
                        _, hi, lo, scale = pieces[n]
                        if not by_pool:
                            weights_lo(dve, n, lo, hi, scale)
                    if isinstance(G, int) and (G, j) == GATE_AT:
                        dve.wait_ge(g_hi, 1)
                        nc.vector.tensor_tensor(gws[1][:], graw[:], gws[0][:].bitcast(F32),
                                                ALU.subtract).then_inc(g_lo, 1)

                def first_lo(n):
                    weights_lo(dve, n, pieces[n][2], pieces[n][1], pieces[n][3])

                dve.sem_inc(res_done, 1)
                ln_stats(dve, 0, 0, x_first)
                ln_rows(dve, 0, 0)
                first_lo(Q)
                z_split_lo(dve, 0, psW)
                first_lo(K)
                first_lo(V)
                qk_split(0, 0)
                for t in range(TPG):
                    v_split(0, 0, t, t % 2)
                    if t == 0:
                        first_lo(3)
                step(0, 0, 0, first=True)
                for j in range(1, PEEL):
                    step(0, j, 0)
                for g in range(1, NGRP):
                    dve.wait_ge(x_in[g - 1], 16)
                with dve.Fori(0, NGRP - 1) as G:
                    for j in range(PEEL, PAIRS):
                        step(G, j, 0)
                    for j in range(PEEL):
                        step(G + 1, j, 0)
                for j in range(PEEL, PAIRS):
                    step(NGRP - 1, j, 1)
                for j in range(PEEL):
                    step(NGRP, j, 1, causal=False)
                with dve.Fori(NGRP, 2 * NGRP - 1) as G:
                    for j in range(PEEL, PAIRS):
                        step(G, j, 1, causal=False)
                    for j in range(PEEL):
                        step(G + 1, j, 1, causal=False, sub=1)
                for j in range(PEEL, PAIRS):
                    step(2 * NGRP - 1, j, 2, causal=False)
                pT_split(STEPS)
                for i in range(2):
                    oT_split(STEPS, 1, i)

            @block.tensor
            def _(pe):
                pe.wait_ge(consts, N_CONST)
                for _ in range(WARM):
                    nc.tensor.matmul(psA[:, 0, 0:P], ident[:], ident[:], start=True, stop=True)

                def qk_project(sub, G, j):
                    jj = j % PAIRS
                    sources = [(zhi, zlo), (chi, clo) if sub == 1 else (zhi, zlo)]
                    if jj == 0:
                        g = G + j // PAIRS
                    half = "lower" if jj < HP else "upper"
                    if jj % HP == 0:
                        wait_lo(pe, f"{'wx'[sub]}q {half}")
                    if j == 1:
                        pe.wait_ge(v_lo, G * 2 * TPG + TPG)
                    elif 2 <= j <= TPG + 1:
                        pe.wait_ge(v_lo, G * 2 * TPG + TPG + j - 1)
                    for n, (hi, lo) in enumerate(sources):
                        if n == K and jj % HP == 0:
                            wait_lo(pe, f"{'wx'[sub]}k {half}")
                            if sub == 1 and jj == 0:
                                pe.wait_ge(c_lo, g + 1 - NGRP)
                        for k in range(KT):
                            if n == Q and jj == 0:
                                pe.wait_ge(z_lo, g * KT + k + 1)
                            c = slice(jj * P, (jj + 1) * P)
                            mm = product(psW[:, n, :], (wh[n][:, k, c], wl[n][:, k, c]), (hi[:, k, :], lo[:, k, :]),
                                         k == 0, k == KT - 1)
                        mm.then_inc(qk_mm, 1)

                def v_project(sub, half, t, bank):
                    hi, lo = (chi, clo) if sub == 1 else (zhi, zlo)
                    c = slice(half * HC, (half + 1) * HC)
                    r = slice(t * P, (t + 1) * P)
                    for k in range(KT):
                        mm = product(psW[:, bank, :], (hi[:, k, r], lo[:, k, r]), (wh[V][:, k, c], wl[V][:, k, c]),
                                     k == 0, k == KT - 1)
                    mm.then_inc(v_mm, 1)

                def v_first_half(sub, G):
                    wait_lo(pe, f"{'wx'[sub]}v lower")
                    for t in range(TPG):
                        if t < 2:
                            pe.wait_ge((q_lo, k_lo)[t], (t + 1) * (G * PAIRS + 1))
                        else:
                            pe.wait_ge(v_lo, G * 2 * TPG + t - 1)
                        v_project(sub, 0, t, t % 2)

                def scores(s, first=False):
                    pe.wait_ge(q_lo, s + 1)
                    pe.wait_ge(k_lo, 2 * s + 2)
                    for i in range(2):
                        if not first:
                            pe.wait_ge(exp_done, 2 * s + i - 1)
                        for b in (2 * i, 2 * i + 1):
                            c = slice(b * P, (b + 1) * P)
                            mm = product(psS[:, i, (b % 2) * D:(b % 2 + 1) * D], tuple(t[:, c] for t in q),
                                         tuple(flat(t[:, b, :, :]) for t in kd),
                                         True, True, skip_group_check=True)
                        mm.then_inc(s_mm, 1)

                def p_transposes(s, first=False):
                    for i in range(2):
                        pe.wait_ge(prob_done, 2 * s + i - 1)
                        if not first:
                            pe.wait_ge(oT_lo, 4 * s - 6 + 2 * i)
                        for n in range(TPG):
                            mm = nc.tensor.transpose(psT[:, i, n * P:(n + 1) * P], prob[:, i * TPG + n, :], ident[:])
                        mm.then_inc(pT_mm, 1)

                def weighted_values(s, j):
                    c = slice(j * P, (j + 1) * P)
                    for i in range(2):
                        pe.wait_ge(pT_lo, 2 * s + i - 1)
                        for b in (2 * i, 2 * i + 1):
                            r = slice((b % 2) * D, (b % 2 + 1) * D)
                            mm = product(psT[:, i, r], tuple(t[:, b, c] for t in v), tuple(t[:, i, r] for t in pT),
                                         True, True, skip_group_check=True)
                        mm.then_inc(oT_mm, 1)

                def out_project(j, parity):
                    for t in range(TPG):
                        mm = product(psA[:, t // 2, (t % 2) * D:(t % 2 + 1) * D], tuple(o[:, parity, t, :] for o in oT),
                                     (wo_hi[:, j, :], wo_lo[:, j, :]), j == 0 and t % 2 == 0, j == PAIRS - 1,
                                     skip_group_check=True)
                    mm.then_inc(proj_mm, 1)

                def step(sub, G, j, after, depth=2):
                    s = G * PAIRS + j
                    scores(s, first=depth == 0)
                    if depth > 0:
                        p_transposes(s, first=depth == 1)
                    if j + 1 < PAIRS:
                        qk_project(sub, G, j + 1)
                    elif after < 2:
                        qk_project(after, G, j + 1)
                    else:
                        pe.wait_ge(gate_in, 32)
                        pe.wait_ge(g_lo, 1)
                        gate_logits(pe, 0)
                    if depth > 0:
                        if j == 1:
                            pe.wait_ge(v_lo, G * 2 * TPG + TPG)
                        if j == HP + 1:
                            pe.wait_ge(v_lo, G * 2 * TPG + 2 * TPG)
                        weighted_values(s, (j - 1) % PAIRS)
                    if depth > 1:
                        if j == 2:
                            pe.wait_ge(res_done, G + 1)
                            wait_lo(pe, f"{'wx'[sub]}r lower")
                        if j == HP + 2:
                            wait_lo(pe, f"{'wx'[sub]}r upper")
                        out_project((j - 2) % PAIRS, j % 2)
                    if j < TPG:
                        pe.wait_ge(q_lo, s + 2)
                        if j == 0:
                            wait_lo(pe, f"{'wx'[sub]}v upper")
                        v_project(sub, 1, j, 0)
                    if j == PAIRS - 2:
                        pe.wait_ge(q_lo, s + 2)
                        pe.wait_ge(k_lo, 2 * (s + 2))
                        z_transposes(pe, G + 1, psW)
                    if j == PAIRS - 1 and after < 2:
                        v_first_half(after, G + 1)

                z_transposes(pe, 0, psW)
                qk_project(0, 0, 0)
                v_first_half(0, 0)
                step(0, 0, 0, 0, depth=0)
                for j in range(1, PEEL):
                    step(0, 0, j, 0, depth=min(j, 2))
                with pe.Fori(0, NGRP - 1) as G:
                    for j in range(PEEL, PAIRS):
                        step(0, G, j, 0)
                    for j in range(PEEL):
                        step(0, G + 1, j, 0)
                for j in range(PEEL, PAIRS):
                    step(0, NGRP - 1, j, 1)
                for j in range(PEEL):
                    step(1, NGRP, j, 1)
                with pe.Fori(NGRP, 2 * NGRP - 1) as G:
                    for j in range(PEEL, PAIRS):
                        step(1, G, j, 1)
                    for j in range(PEEL):
                        step(1, G + 1, j, 1)
                for j in range(PEEL, PAIRS):
                    step(1, 2 * NGRP - 1, j, 2)
                p_transposes(STEPS)
                out_project(PAIRS - 2, 0)
                wait_lo(pe, "w1 lower")
                wait_lo(pe, "w1 upper")
                pe.wait_ge(exp_done, 2 * STEPS)
                for k in range(KT):
                    hidden_half(w1s, 0, 0, k)
                weighted_values(STEPS, PAIRS - 1)
                for k in range(KT):
                    mm = hidden_half(w1s, 0, 1, k)
                mm.then_inc(ab_mm, 1)
                pe.wait_ge(oT_lo, 4 * STEPS)
                out_project(PAIRS - 1, 1)

        ffn = ExitStack()
        with ffn:
            def fb(name, shape, dt=F32):
                return sb(name, shape, dt, ffn)

            wouts = [fb(f"wout_{n}", [P, HT, D], F32R) for n in ("hi", "lo")]
            wins = [fb(f"win_{n}", [P, KT, 2 * HID], F32R) for n in ("hi", "lo")]
            w2s = [fb(f"w2_{n}", [P, HT, NE * D], F32R) for n in ("hi", "lo")]
            earlier = fb("earlier", [P, NE, NE])
            hids = [fb(f"hid_{n}", [P, 2 * HT, GT], F32R) for n in ("hi", "lo")]
            silu = fb("silu", [P, 2, GT])
            h = fb("h", [P, 2, GT])
            logitsT = fb("logitsT", [NG, GT])
            logits = fb("logits", [P, TPG, NG])
            gmax = fb("gmax", [P, TPG])
            emax = fb("emax", [P, TPG, GROUPS])
            probs = fb("probs", [P, TPG, NG])
            gsum = fb("gsum", [P, TPG])
            esum = fb("esum", [P, TPG, GROUPS])
            chosen = fb("chosen", [P, TPG, GROUPS])
            coef = fb("coef", [P, TPG, GROUPS])
            above = fb("above", [P, TPG, NE, NE])
            ties = fb("ties", [P, TPG, NE, NE])
            rank = fb("rank", [P, TPG, NE])
            wse = fb("wse", [P, TPG, NE])
            acc = fb("acc", [P, 2, D])
            fin = fb("fin", [P, FIN, D])
            OB = [psT[:, 0, :], psT[:, 1, :], psA[:, 0, :], psA[:, 1, :]]
            GSTEPS = 19
            N0 = len(pieces)
            parts = [(wins[0][:], wins[1][:])] + \
                    [tuple(w[:, k, :].rearrange("p (e n) -> p e n", e=NE) for w in w2s) for k in range(HT)] + \
                    [(wouts[0][:], wouts[1][:])]
            late = [(src, *hl) for src, hl in zip(late_sources, parts)]
            LATE_HI_AT = {0: (1,), 1: (2,), 3: (3,), 4: (4,), 6: (5,)}
            LATE_LO_AT = {2: (2,), 5: (4,), 6: (5,)}

            def late_name(i):
                return PIECES[N0 + i]

            block2 = ffn.enter_context(nc.Block())

            @block2.sync
            def _(sp):
                for slot in stored:
                    sp.sem_inc(slot, 16)
                for i in range(STAGES, len(late)):
                    wait_lo(sp, late_name(i - STAGES))
                    sp.dma_start(piece(N0 + i, late[i][0].shape), late[i][0]).then_inc(stage_in[(N0 + i) % STAGES], 16)
                with sp.Fori(0, NGRP) as g:
                    for t in range(TPG):
                        sp.wait_ge(fin_done, g * TPG + t + 1)
                        sp.dma_start(out[bass.ds((g * TPG + t) * P, P), :], fin[:, t % FIN, :]).then_inc(stored[t % FIN], 16)
                for slot in stored:
                    sp.wait_ge(slot, 16 * (B // FIN + 1))

            @block2.gpsimd
            def _(pool):
                nc.gpsimd.memset(earlier[:], 1.0).then_inc(ffn_ones, 1)
                pool.wait_ge(ffn_ones, 1)
                nc.gpsimd.affine_select(out=earlier[:], in_=earlier[:], compare_op=ALU.is_gt, fill=0.0, base=0,
                                        pattern=[[1, NE], [-1, NE]], channel_multiplier=0).then_inc(ffn_consts, 1)
                for i, (_, hi, lo) in enumerate(late):
                    if late_name(i) in BY_POOL:
                        weights_lo_pool(pool, N0 + i, lo, hi)
                with pool.Fori(2 * NGRP + 1, 3 * NGRP) as g:
                    ln_scale(pool, g)

            @block2.scalar
            def _(act):
                def group(g, first=False):
                    if not first:
                        z_split_hi(act, g + L0, psS)
                    for m in range(MT):
                        act.wait_ge(ab_mm, g * MT + m + 1)
                        if not (first and m < 2):
                            act.wait_ge(h_done, g * MT + m - 1)
                        nc.scalar.activation(silu[:, m % 2, :], AB[2 * (m % 2)], ACT.Silu).then_inc(silu_done, 1)
                        if m >= 1:
                            split(g, m - 1)
                        for i in LATE_HI_AT.get(m, ()) if first else ():
                            weights_hi(act, N0 + i, late[i][1])
                    split(g, MT - 1)
                    act.wait_ge(gate_step, g * GSTEPS + 4)
                    nc.scalar.activation(flat(probs[:]), flat(logits[:]), ACT.Exp).then_inc(gate_exp, 1)
                    act.preload_act_table(ACT.Silu)

                def split(g, m):
                    act.wait_ge(h_done, g * MT + m + 1)
                    nc.scalar.activation(hids[0][:, m, :], h[:, m % 2, :], ACT.Copy).then_inc(h_hi, 1)

                weights_hi(act, N0, late[0][1])
                group(0, first=True)
                with act.Fori(1, NGRP) as g:
                    group(g)

            @block2.vector
            def _(dve):
                def gating(g):
                    count = [0]

                    def link(ins):
                        count[0] += 1
                        ins.then_inc(gate_step, 1)

                    def linked():
                        dve.wait_ge(gate_step, g * GSTEPS + count[0])

                    def wide(ap, n):
                        return ap.unsqueeze(len(ap.shape)).broadcast_to([*ap.shape, n])

                    lg = logits[:, :, 0:GROUPS]
                    le = logits[:, :, GROUPS:NG].rearrange("p t (g e) -> p t g e", g=GROUPS)
                    pg = probs[:, :, 0:GROUPS]
                    pe_ = probs[:, :, GROUPS:NG]
                    pe4 = pe_.rearrange("p t (g e) -> p t g e", g=GROUPS)
                    dve.wait_ge(gate_copied, g + 1)
                    link(nc.vector.tensor_reduce(gmax[:], lg, AX.X, ALU.max))
                    link(nc.vector.tensor_reduce(emax[:], le, AX.X, ALU.max))
                    linked()
                    link(nc.vector.tensor_tensor(lg, lg, wide(gmax[:], GROUPS), ALU.subtract))
                    link(nc.vector.tensor_tensor(le, le, wide(emax[:], PER_GROUP), ALU.subtract))
                    dve.wait_ge(gate_exp, g + 1)
                    link(nc.vector.tensor_reduce(gsum[:], pg, AX.X, ALU.add))
                    link(nc.vector.tensor_reduce(esum[:], pe4, AX.X, ALU.add))
                    linked()
                    link(nc.vector.reciprocal(gsum[:], gsum[:]))
                    link(nc.vector.reciprocal(esum[:], esum[:]))
                    linked()
                    link(nc.vector.tensor_tensor(pg, pg, wide(gsum[:], GROUPS), ALU.mult))
                    linked()
                    link(nc.vector.tensor_tensor(chosen[:, :, 0], pg[:, :, 0], pg[:, :, 1], ALU.is_ge))
                    link(nc.vector.tensor_tensor(chosen[:, :, 1], pg[:, :, 0], pg[:, :, 1], ALU.is_lt))
                    linked()
                    link(nc.vector.tensor_tensor(chosen[:], chosen[:], pg, ALU.mult))
                    linked()
                    link(nc.vector.tensor_tensor(coef[:], chosen[:], esum[:], ALU.mult))
                    linked()
                    link(nc.vector.tensor_tensor(pe4, pe4, wide(coef[:], PER_GROUP), ALU.mult))
                    linked()
                    this = wide(pe_, NE)
                    other = pe_.unsqueeze(2).broadcast_to([P, TPG, NE, NE])
                    link(nc.vector.tensor_tensor(above[:], other, this, ALU.is_gt))
                    link(nc.vector.tensor_tensor(ties[:], other, this, ALU.is_equal))
                    linked()
                    link(nc.vector.tensor_tensor(ties[:], ties[:],
                                                 earlier[:].unsqueeze(1).broadcast_to([P, TPG, NE, NE]), ALU.mult))
                    linked()
                    link(nc.vector.tensor_tensor(above[:], above[:], ties[:], ALU.add))
                    linked()
                    link(nc.vector.tensor_reduce(rank[:], above[:], AX.X, ALU.add))
                    linked()
                    assert count[0] == GSTEPS
                    nc.vector.scalar_tensor_tensor(wse[:], rank[:], TOP_K - 0.5, pe_, ALU.is_lt,
                                                   ALU.mult).then_inc(wse_done, 1)
                    dve.wait_ge(wse_done, g + 1)

                def hidden(g, first=False):
                    dve.wait_ge(gate_mm, g + 1)
                    nc.vector.tensor_scalar(logitsT[:], AB[2][0:NG, :], gbias[:, 0:1], None,
                                            ALU.add).then_inc(gate_biased, 1)
                    dve.wait_ge(gate_T, g + 1)
                    nc.vector.tensor_copy(flat(logits[:]), AB[3][:, 0:TPG * NG]).then_inc(gate_copied, 1)
                    if first:
                        residual(dve, L0 - 1, 1)
                    for m in range(MT):
                        dve.wait_ge(silu_done, g * MT + m + 1)
                        if not (first and m < 2):
                            dve.wait_ge(h_lo, g * MT + m - 1)
                        nc.vector.tensor_tensor(h[:, m % 2, :], AB[2 * (m % 2) + 1], silu[:, m % 2, :],
                                                ALU.mult).then_inc(h_done, 1)
                        if m >= 1:
                            split(g, m - 1)
                        for i in LATE_LO_AT.get(m, ()) if first else ():
                            weights_lo(dve, N0 + i, late[i][2], late[i][1])
                    split(g, MT - 1)

                def split(g, m):
                    dve.wait_ge(h_hi, g * MT + m + 1)
                    nc.vector.tensor_tensor(hids[1][:, m, :], h[:, m % 2, :], hids[0][:, m, :].bitcast(F32),
                                            ALU.subtract).then_inc(h_lo, 1)

                def combine(g, t):
                    n0, a0 = g * TPG * OUTS + t * OUTS, (g * TPG + t + 1) * NE
                    chains = [fin[:, t % FIN, :], acc[:, t % 2, :]]
                    for c in range(OUTS - 1):
                        dve.wait_ge(out_mm, n0 + c + 1)
                        for i in range(2):
                            e = 2 * c + i
                            src, w, dst = OB[(t * OUTS + c) % 4][:, i * D:(i + 1) * D], wse[:, t, e:e + 1], chains[i]
                            if c:
                                dve.wait_ge(acc_done, a0 + e - 1)
                            if c == 0 and i == 0:
                                dve.wait_ge(stored[t % FIN], (g * (TPG // FIN) + t // FIN + 1) * 16)
                                ins = nc.vector.scalar_tensor_tensor(dst, src, w, row_tile(g, t), ALU.mult, ALU.add)
                            elif c == 0:
                                ins = nc.vector.tensor_scalar(dst, src, w, None, ALU.mult)
                            else:
                                ins = nc.vector.scalar_tensor_tensor(dst, src, w, dst, ALU.mult, ALU.add)
                            ins.then_inc(acc_done, 1)
                    dve.wait_ge(out_mm, n0 + OUTS)
                    dve.wait_ge(acc_done, a0 + NE)
                    nc.vector.tensor_tensor(chains[1], OB[(t * OUTS + OUTS - 1) % 4][:, 0:D], chains[1],
                                            ALU.add).then_inc(out_used, 1)
                    dve.wait_ge(out_used, g * TPG + t + 2)
                    nc.vector.tensor_tensor(chains[0], chains[0], chains[1], ALU.add).then_inc(fin_done, 1)

                def outputs(g, more=True):
                    combine(g, 0)
                    if more:
                        ln_stats(dve, g + 1 + L0, g + 1)
                    combine(g, 1)
                    if more:
                        ln_rows(dve, g + 1 + L0, g + 1)
                    combine(g, 2)
                    if more:
                        z_split_lo(dve, g + 1 + L0, psS)
                    combine(g, 3)

                dve.sem_inc(acc_done, NE)
                dve.sem_inc(out_used, 1)
                dve.wait_ge(ffn_consts, 1)
                hidden(0, first=True)
                dve.wait_ge(res_done, L0 + 1)
                gating(0)
                with dve.Fori(0, NGRP - 1) as g:
                    outputs(g)
                    hidden(g + 1)
                    gating(g + 1)
                outputs(NGRP - 1, more=False)

            @block2.tensor
            def _(pe):
                def hidden(g, first=False):
                    if not first:
                        gate_logits(pe, g)
                    for m in range(MT):
                        ws = w1s if m < HT else wins
                        if m == HT:
                            wait_lo(pe, "win")
                        if m == 1:
                            pe.wait_ge(gate_copied, g + 1)
                        if m >= 2:
                            pe.wait_ge(h_done, g * MT + m - 1)
                        for half in range(2):
                            for k in range(KT):
                                if m == 0 and (half, k) == (1, 0):
                                    pe.wait_ge(gate_biased, g + 1)
                                if not (first and m == 0):
                                    mm = hidden_half(ws, m, half, k)
                                if m == 0 and (half, k) == (1, 0):
                                    for t in range(TPG):
                                        tr = nc.tensor.transpose(AB[3][:, t * NG:(t + 1) * NG],
                                                                 logitsT[:, t * P:(t + 1) * P], ident[0:NG, 0:NG])
                                    tr.then_inc(gate_T, 1)
                        if not (first and m == 0):
                            mm.then_inc(ab_mm, 1)

                def outputs(g, more=True):
                    for t in range(TPG):
                        r = slice(t * P, (t + 1) * P)
                        for c in range(OUTS):
                            n = t * OUTS + c
                            shared = c == OUTS - 1
                            if t == 0:
                                if c == 0:
                                    wait_lo(pe, "w2 2")
                                    wait_lo(pe, "w2 3")
                                    pe.wait_ge(h_lo, g * MT + HT)
                                if shared:
                                    wait_lo(pe, "wout")
                                    pe.wait_ge(h_lo, g * MT + MT)
                            back, place = (n - 4) // OUTS, (n - 4) % OUTS
                            if place == OUTS - 1:
                                pe.wait_ge(out_used, g * TPG + back + 2)
                            else:
                                pe.wait_ge(acc_done, (g * TPG + back + 1) * NE + 2 * place + 2)
                            for k in range(HT):
                                m = HT + k if shared else k
                                lhs = (hids[0][:, m, r], hids[1][:, m, r])
                                cols_ = slice(c * 2 * D, (c + 1) * 2 * D)
                                rhs = tuple(w[:, k, :] for w in wouts) if shared else tuple(w[:, k, cols_] for w in w2s)
                                dst = OB[n % 4][:, 0:D] if shared else OB[n % 4]
                                mm = product(dst, lhs, rhs, k == 0, k == HT - 1)
                            mm.then_inc(out_mm, 1)
                        if t == 2 and more:
                            pe.wait_ge(h_done, (g + 1) * MT)
                            z_transposes(pe, g + 1 + L0, psS)

                hidden(0, first=True)
                pe.wait_ge(res_done, L0 + 1)
                with pe.Fori(0, NGRP - 1) as g:
                    outputs(g)
                    hidden(g + 1)
                outputs(NGRP - 1, more=False)


def kernel(**inputs):
    import numpy as _np
    import concourse.bacc as _bacc
    from concourse import mybir as _mybir
    from concourse.bass_utils import run_bass_kernel_spmd as _run

    def c(a):
        return _np.ascontiguousarray(a)

    a = {k: _np.asarray(v) for k, v in inputs.items()}
    tokens = a["x"].shape[0] * a["x"].shape[1]
    d = a["x"].shape[2]
    w2 = a["L0_ffn_w2"]
    arrays = {
        "x": c(a["x"].reshape(tokens, d)),
        "ctxT": c(a["ctx_1024"].reshape(tokens, d).T),
        "wq": c(a["L0_attn_Wq"]), "wk": c(a["L0_attn_Wk"]), "wv": c(a["L0_attn_Wv"]), "wr": c(a["L0_attn_Wr"]),
        "xq": c(a["L0_xattn_w_q"]), "xk": c(a["L0_xattn_w_k"]), "xv": c(a["L0_xattn_w_v"]), "xr": c(a["L0_xattn_w_o"]),
        "w1": c(a["L0_ffn_w1"].T), "win": c(a["L0_ffn_w_in"].T), "wout": c(a["L0_ffn_w_out"].T),
        "w2": c(w2.transpose(2, 0, 1).reshape(w2.shape[2], w2.shape[0] * w2.shape[1])),
        "wgate": c(_np.concatenate([a["L0_ffn_wg"], a["L0_ffn_we"]], 0).T),
        "bgate": c(_np.concatenate([a["L0_ffn_gb"], a["L0_ffn_eb"]])[:, None]),
    }
    nc = _bacc.Bacc("TRN2", target_bir_lowering=False, num_devices=1)
    args = [nc.dram_tensor(n, v.shape, _mybir.dt.from_np(v.dtype), kind="ExternalInput").ap() for n, v in arrays.items()]
    out = nc.dram_tensor("out", (tokens, d), _mybir.dt.float32, kind="ExternalOutput").ap()
    build(nc, *args, out)
    r = _run(nc, [arrays], core_ids=[0])
    return r.results[0]["out"].reshape(a["x"].shape)
```
